# Optimizing a Trainium2 kernel written in Bass

```python
import numpy as np
import jax
import jax.numpy as jnp

def _softmax(x, axis=-1):
    return jax.nn.softmax(x, axis=axis)

def _gelu(x):
    return jax.nn.gelu(x, approximate=True)

def _silu(x):
    return jax.nn.silu(x)

def _sigmoid(x):
    return jax.nn.sigmoid(x)

def _layernorm(x, axis=-1, eps=1e-05):
    m = jnp.mean(x, axis=axis, keepdims=True)
    v = jnp.var(x, axis=axis, keepdims=True)
    return (x - m) / jnp.sqrt(v + eps)

def _scatter_add(tgt, idx, src, axis=0):
    return tgt.at[idx].add(src)

def _segment_sum(src, seg, n):
    return jax.ops.segment_sum(src, seg, n)
kernel_name = 'mk_decoder_postln_d1_seqx_r8_3e6045'

def setup_inputs(seed: int=0):
    np.random.seed(seed)
    _w = jnp.asarray

    def _rec_inputs():
        import jax
        import jax.numpy as jnp
        _rk = jax.random.key(seed)
        x = -0.000125 + 0.9999 * jax.random.normal(jax.random.fold_in(_rk, 1), (4, 256, 256), jnp.float32)
        _lenS = 256 - jax.random.randint(jax.random.fold_in(_rk, 7), (4,), 0, max(1, 256 // 4) + 1, jnp.int32)
        _lenS2 = 256 - jax.random.randint(jax.random.fold_in(_rk, 8), (4,), 0, max(1, 256 // 4) + 1, jnp.int32)
        itok_BxS_13_99985 = jax.random.randint(jax.random.fold_in(_rk, 11), (4, 256), 13, 99986, jnp.int32)
        _ctx_2048P = jax.random.normal(jax.random.fold_in(_rk, 12), (4, 16, 256), jnp.float32)
        _ctx_2048c = jax.random.dirichlet(jax.random.fold_in(_rk, 512), 0.3 * jnp.ones((16,), jnp.float32), (4, 256))
        _ctx_2048t = jnp.einsum('bsk,bkd->bsd', _ctx_2048c, _ctx_2048P)
        _ctx_2048t = _ctx_2048t * jax.lax.rsqrt(jnp.mean(jnp.square(_ctx_2048t)) + 1e-12) * 0.953939
        ctx_2048 = 6.82029e-06 + 0.0200006 * (_ctx_2048t + 0.3 * jax.random.normal(jax.random.fold_in(_rk, 612), (4, 256, 256), jnp.float32))
        return (x, itok_BxS_13_99985, ctx_2048)
    x, itok_BxS_13_99985, ctx_2048 = _rec_inputs()

    def _L0_attn_setup():
        import jax, jax.numpy as jnp
        import numpy as np
        DIM, H, P, N = (256, 32, 64, 128)
        K = 4

        def _causal_conv(u, w):
            T = u.shape[1]
            up = jnp.pad(u, ((0, 0), (K - 1, 0), (0, 0), (0, 0)))
            out = jnp.zeros_like(u)
            for k in range(K):
                out = out + up[:, k:k + T] * w[:, :, k]
            return out
        key = jax.random.key(seed)
        ks = jax.random.split(key, 8)
        proj_dim = 2 * H * P + 2 * H * N + H
        x = jax.random.normal(ks[0], (2, 256, DIM), dtype=jnp.float32)
        Win = jax.random.normal(ks[1], (proj_dim, DIM), dtype=jnp.float32) * 0.02
        Wout = jax.random.normal(ks[2], (DIM, H * P), dtype=jnp.float32) * 0.02
        A_log = jnp.linspace(-3.0, -1.0, H, dtype=jnp.float32)
        dt_bias = jnp.zeros((H,), dtype=jnp.float32)
        conv_w_x = jax.random.normal(ks[3], (H, P, K), dtype=jnp.float32) * 0.1
        conv_w_b = jax.random.normal(ks[4], (H, N, K), dtype=jnp.float32) * 0.1
        conv_w_c = jax.random.normal(ks[5], (H, N, K), dtype=jnp.float32) * 0.1
        return {'x': x, 'Win': Win, 'Wout': Wout, 'A_log': A_log, 'dt_bias': dt_bias, 'conv_w_x': conv_w_x, 'conv_w_b': conv_w_b, 'conv_w_c': conv_w_c}
    _L0_attn_all = _L0_attn_setup()
    _L0_attn_in = {k: v for k, v in _L0_attn_all.items() if k in ('Win', 'Wout', 'A_log', 'dt_bias', 'conv_w_x', 'conv_w_b', 'conv_w_c')}
    del _L0_attn_all

    def _L0_xattn_setup():
        import jax, jax.numpy as jnp
        import numpy as np
        B, S, D = (4, 512, 256)
        E = 4
        F = 1024 // E
        VOCAB = 12500
        key = jax.random.key(seed)
        k1, k2, k3, k4, k5 = jax.random.split(key, 5)
        hidden_states = jax.random.normal(k1, (B, S, D), dtype=jnp.float32)
        token_ids = jax.random.randint(k2, (B, S), 0, VOCAB, dtype=jnp.int64)
        Wg = jax.random.normal(k3, (E, F, D), dtype=jnp.float32) * 0.02
        Wu = jax.random.normal(k4, (E, F, D), dtype=jnp.float32) * 0.02
        Wd = jax.random.normal(k5, (E, D, F), dtype=jnp.float32) * 0.02
        return {'hidden_states': hidden_states, 'token_ids': token_ids, 'Wg': Wg, 'Wu': Wu, 'Wd': Wd}
    _L0_xattn_all = _L0_xattn_setup()
    _L0_xattn_in = {k: v for k, v in _L0_xattn_all.items() if k in ()}
    del _L0_xattn_all

    def _L0_ffn_setup():
        import jax, jax.numpy as jnp
        import numpy as np
        E = 16
        K = 2
        D = 256
        F = 176
        B, S = (4, 256)

        def _swiglu(x, wg, wu, wd):
            return jax.nn.silu(x @ wg.T) * (x @ wu.T) @ wd.T
        key = jax.random.key(seed)
        ks = jax.random.split(key, 8)
        sc = 0.02
        return {'x': jax.random.normal(ks[0], (B, S, D), jnp.float32), 'gate_w': jax.random.normal(ks[1], (E, D), jnp.float32) * sc, 'w_gate': jax.random.normal(ks[2], (E, F, D), jnp.float32) * sc, 'w_up': jax.random.normal(ks[3], (E, F, D), jnp.float32) * sc, 'w_down': jax.random.normal(ks[4], (E, D, F), jnp.float32) * sc, 'sw_gate': jax.random.normal(ks[5], (F, D), jnp.float32) * sc, 'sw_up': jax.random.normal(ks[6], (F, D), jnp.float32) * sc, 'sw_down': jax.random.normal(ks[7], (D, F), jnp.float32) * sc, 'expert_bias': jnp.zeros((E,), jnp.float32)}
    _L0_ffn_all = _L0_ffn_setup()
    _L0_ffn_in = {k: v for k, v in _L0_ffn_all.items() if k in ('gate_w', 'w_gate', 'w_up', 'w_down', 'sw_gate', 'sw_up', 'sw_down', 'expert_bias')}
    del _L0_ffn_all
    return {'x': x, 'itok_BxS_13_99985': itok_BxS_13_99985, 'ctx_2048': ctx_2048, 'L0_attn_Win': _L0_attn_in['Win'], 'L0_attn_Wout': _L0_attn_in['Wout'], 'L0_attn_A_log': _L0_attn_in['A_log'], 'L0_attn_dt_bias': _L0_attn_in['dt_bias'], 'L0_attn_conv_w_x': _L0_attn_in['conv_w_x'], 'L0_attn_conv_w_b': _L0_attn_in['conv_w_b'], 'L0_attn_conv_w_c': _L0_attn_in['conv_w_c'], 'L0_ffn_gate_w': _L0_ffn_in['gate_w'], 'L0_ffn_w_gate': _L0_ffn_in['w_gate'], 'L0_ffn_w_up': _L0_ffn_in['w_up'], 'L0_ffn_w_down': _L0_ffn_in['w_down'], 'L0_ffn_sw_gate': _L0_ffn_in['sw_gate'], 'L0_ffn_sw_up': _L0_ffn_in['sw_up'], 'L0_ffn_sw_down': _L0_ffn_in['sw_down'], 'L0_ffn_expert_bias': _L0_ffn_in['expert_bias']}

def reference(x, itok_BxS_13_99985, ctx_2048, L0_attn_Win, L0_attn_Wout, L0_attn_A_log, L0_attn_dt_bias, L0_attn_conv_w_x, L0_attn_conv_w_b, L0_attn_conv_w_c, L0_ffn_gate_w, L0_ffn_w_gate, L0_ffn_w_up, L0_ffn_w_down, L0_ffn_sw_gate, L0_ffn_sw_up, L0_ffn_sw_down, L0_ffn_expert_bias):
    import jax
    import jax.numpy as jnp

    def _L0_attn_ref(x, Win, Wout, A_log, dt_bias, conv_w_x, conv_w_b, conv_w_c):
        import jax, jax.numpy as jnp
        import numpy as np
        DIM, H, P, N = (256, 32, 64, 128)
        K = 4

        def _causal_conv(u, w):
            T = u.shape[1]
            up = jnp.pad(u, ((0, 0), (K - 1, 0), (0, 0), (0, 0)))
            out = jnp.zeros_like(u)
            for k in range(K):
                out = out + up[:, k:k + T] * w[:, :, k]
            return out
        B, T, _ = x.shape
        proj = x @ Win.T
        x_ssm = proj[..., :H * P].reshape(B, T, H, P)
        z = proj[..., H * P:2 * H * P].reshape(B, T, H, P)
        Bm = proj[..., 2 * H * P:2 * H * P + H * N].reshape(B, T, H, N)
        Cm = proj[..., 2 * H * P + H * N:2 * H * P + 2 * H * N].reshape(B, T, H, N)
        dt_raw = proj[..., 2 * H * P + 2 * H * N:]
        dt = jax.nn.softplus(dt_raw + dt_bias)
        xc = jax.nn.silu(_causal_conv(x_ssm, conv_w_x))
        Bc = jax.nn.silu(_causal_conv(Bm, conv_w_b))
        Cc = jax.nn.silu(_causal_conv(Cm, conv_w_c))
        A = -jnp.exp(A_log)
        decay = jnp.exp(dt * A)
        dtx = dt[..., None] * xc

        def step(h, inp):
            dec_t, dtx_t, B_t, C_t = inp
            h = dec_t[..., None, None] * h + dtx_t[..., None] * B_t[:, :, None, :]
            y = jnp.einsum('bhpn,bhn->bhp', h, C_t)
            return (h, y)
        h0 = jnp.zeros((B, H, P, N), dtype=x.dtype)
        xs = (jnp.moveaxis(decay, 1, 0), jnp.moveaxis(dtx, 1, 0), jnp.moveaxis(Bc, 1, 0), jnp.moveaxis(Cc, 1, 0))
        _, ys = jax.lax.scan(step, h0, xs)
        y = jnp.moveaxis(ys, 0, 1)
        y = y * jax.lax.rsqrt(jnp.mean(y * y, axis=-1, keepdims=True) + 1e-06)
        y = y * jax.nn.silu(z)
        return y.reshape(B, T, H * P) @ Wout.T

    def _L0_xattn_ref(hidden_states, token_ids, Wg, Wu, Wd):
        import jax, jax.numpy as jnp
        import numpy as np
        B, S, D = (4, 512, 256)
        E = 4
        F = 1024 // E
        VOCAB = 12500
        tokens_per_expert = VOCAB // E
        tid = jnp.clip(token_ids, 0, VOCAB - 1)
        expert_ids = jnp.minimum(tid // tokens_per_expert, E - 1)
        out = jnp.zeros_like(hidden_states)
        for e in range(E):
            g = jax.nn.silu(jnp.einsum('bsd,fd->bsf', hidden_states, Wg[e]))
            u = jnp.einsum('bsd,fd->bsf', hidden_states, Wu[e])
            y = jnp.einsum('bsf,df->bsd', g * u, Wd[e])
            out = jnp.where((expert_ids == e)[..., None], y, out)
        return out

    def _L0_ffn_ref(x, gate_w, w_gate, w_up, w_down, sw_gate, sw_up, sw_down, expert_bias):
        import jax, jax.numpy as jnp
        import numpy as np
        E = 16
        K = 2
        D = 256
        F = 176
        B, S = (4, 256)

        def _swiglu(x, wg, wu, wd):
            return jax.nn.silu(x @ wg.T) * (x @ wu.T) @ wd.T
        b, s, d = x.shape
        flat = x.reshape(-1, d)
        logits = flat @ gate_w.T
        probs = jax.nn.softmax(logits, axis=-1)
        biased = logits + expert_bias
        _, top_idx = jax.lax.top_k(biased, K)
        top_w = jnp.take_along_axis(probs, top_idx, axis=-1)
        top_w = top_w / jnp.sum(top_w, axis=-1, keepdims=True)
        combine = jnp.sum(jax.nn.one_hot(top_idx, E, dtype=flat.dtype) * top_w[..., None], axis=1)
        out = jnp.zeros_like(flat)
        for e in range(E):
            out = out + combine[:, e:e + 1] * _swiglu(flat, w_gate[e], w_up[e], w_down[e])
        out = out + _swiglu(flat, sw_gate, sw_up, sw_down)
        return out.reshape(b, s, d)
    x = _layernorm(x + _L0_attn_ref(x, L0_attn_Win, L0_attn_Wout, L0_attn_A_log, L0_attn_dt_bias, L0_attn_conv_w_x, L0_attn_conv_w_b, L0_attn_conv_w_c), axis=-1)
    x = _layernorm(x + _L0_xattn_ref(x, itok_BxS_13_99985, ctx_2048, ctx_2048, ctx_2048), axis=-1)
    x = _layernorm(x + _L0_ffn_ref(x, L0_ffn_gate_w, L0_ffn_w_gate, L0_ffn_w_up, L0_ffn_w_down, L0_ffn_sw_gate, L0_ffn_sw_up, L0_ffn_sw_down, L0_ffn_expert_bias), axis=-1)
    return x

_drawn_inputs = setup_inputs


def setup_inputs(seed=0):
    import zlib

    import numpy as np

    out = dict(_drawn_inputs(seed))
    spreads = {'L0_attn_dt_bias': (0.0, 0.8), 'L0_ffn_expert_bias': (0.0, 0.8)}
    factors = {'L0_ffn_gate_w': 6.203,
     'L0_ffn_w_gate': 5.742,
     'L0_ffn_w_up': 5.654,
     'L0_ffn_w_down': 5.648,
     'L0_ffn_sw_gate': 4.119,
     'L0_ffn_sw_up': 4.064,
     'L0_ffn_sw_down': 4.09}
    for name, (base, spread) in spreads.items():
        noise = np.random.default_rng([zlib.crc32(name.encode()), seed]).standard_normal(out[name].shape)
        drawn = base * np.exp(spread * noise) if base else spread * noise
        out[name] = jnp.asarray(drawn.astype(out[name].dtype))
    for name, factor in factors.items():
        out[name] = (out[name] * factor).astype(out[name].dtype)
    return out
```

```python
import concourse.bass as bass
from concourse import mybir
from contextlib import ExitStack

F32 = mybir.dt.float32
F32R = mybir.dt.float32r
BF16 = mybir.dt.bfloat16
I32 = mybir.dt.int32
ALU = mybir.AluOpType
ACT = mybir.ActivationFunctionType
AX = mybir.AxisListType

P = 128
NB, T, D = 4, 256, 256
NT = NB * T
TB = NT // P
KD = D // P
H, HP, N, TAPS = 32, 64, 128, 4
NPAIR = H // 2
NTILE = 6
NCONV = NTILE - 1
PW = NTILE * P
RAWW = KD * PW + NCONV * TAPS
UNITS = 2 * NB
SC = T + P
EX = 4
VOCAB = 12500
TPE = VOCAB // EX
NE, FF = 16, 176
FH = FF // 2
ME = NE + 1
RW = KD * 2 * FF + 2 * D
NEG = -1.0e30
PAD = -3.0e38
HIT = 3.0e38
LN_EPS = 1e-5
RMS_EPS = 1e-6


def build_layer(nc, xT, x, winT, wdtT, a_log, dt_bias, woutT, ids, ctxT, gateT, ebias, wexp, out):
    cneg = nc.dram_tensor("cneg_scratch", (3, H, NT), BF16, kind="Internal").ap()
    cpos = nc.dram_tensor("cpos_scratch", (3, H, NT), BF16, kind="Internal").ap()

    with ExitStack() as ctx:
        def sb(name, shape, dt=F32):
            return ctx.enter_context(nc.sbuf_tensor(name, shape, dt))

        def sem(name):
            return ctx.enter_context(nc.semaphore(name))

        ps = ctx.enter_context(nc.psum_tensor("ps", [P, 8, 512], F32))

        x_hi = sb("x_hi", [P, KD, NT], F32R)
        x_lo = sb("x_lo", [P, KD, NT], F32R)
        w_raw = sb("w_raw", [P, 2, RAWW])
        w_hi = sb("w_hi", [P, 2, KD * PW], F32R)
        w_lo = sb("w_lo", [P, 2, KD * PW], F32R)
        conv = sb("conv", [P, 2, NCONV, NT])
        z_gate = sb("z_gate", [P, 2, NT])
        xs = sb("xs", [P, TB, P])
        decay = sb("decay", [P, 2, SC])
        scores = sb("scores", [P, 2, SC])
        y_all = sb("y_all", [P, NPAIR, NT])
        y_gated = sb("y_gated", [P, 512])
        y_sq = sb("y_sq", [P, 512])
        y_rs = sb("y_rs", [P, 512])
        cum = sb("cum", [P, 2, 2, 2 * NT], BF16)
        cum_l = cum[0:6, 0, :, :]
        cum_r = cum[0:6, 1, :, :]
        dt_tok = sb("dt_tok", [P, TB, H])
        ident = sb("ident", [P, P])
        ident_b = sb("ident_b", [P, P], BF16)
        mask = sb("mask", [P, SC], BF16)
        mean_w = sb("mean_w", [P, P])
        eps_rms = sb("eps_rms", [P, 1])
        eps_ln = sb("eps_ln", [P, 1])
        zero = sb("zero", [P, 1])
        head_c = sb("head_c", [H, 3])

        xT_raw = y_all[:, 0:2, :]
        wdt = y_all[:, 2, 0:KD * H].rearrange("p (k h) -> p k h", k=KD)
        dt_z, dt_e, dt_l, dt_ch, dt_da, dt_cum, dt_r = (y_all[0:H, 3 + i, :] for i in range(7))
        cum_b = y_all[0:H, 10:13, :].bitcast(BF16).rearrange("p a t -> p (a t)")[:, 0:6 * NT].rearrange(
            "p (a t) -> p a t", a=6)

        conv_f = conv[:, :, :, :].rearrange("p a b t -> p (a b t)")
        at = [0]

        def carve(n):
            at[0] += n
            return conv_f[:, at[0] - n:at[0]]
        x_tok = carve(TB * D).rearrange("p (b d) -> p b d", b=TB)
        x1 = carve(TB * D).rearrange("p (b d) -> p b d", b=TB)
        x2 = x_tok
        x1T = carve(KD * NT).rearrange("p (k t) -> p k t", k=KD)
        ctx_w = carve(EX * KD * D).rearrange("p (e k f) -> p e k f", e=EX, k=KD)
        xm = w_raw[:, :, 0:KD * 512].rearrange("p r (k t) -> p r k t", k=KD)
        emask = carve(EX * NT // 2).bitcast(BF16).rearrange("p (e t) -> p e t", e=EX)
        wo_sb = cum[:, :, :, :].bitcast(F32).rearrange("p a b t -> p (a b t)").rearrange("p (i d) -> p i d", i=NPAIR)
        gm = y_all[:, 0:4, :].rearrange("p e (k t) -> p e k t", k=KD)
        g_sb = y_all[:, 4, :].rearrange("p (k t) -> p k t", k=KD)
        sg_sb = y_all[:, 5, :].rearrange("p (k t) -> p k t", k=KD)
        x2T = y_all[:, 6:8, :]
        exp_raw = y_all[:, 8:12, :].rearrange("p a t -> p (a t)")[:, 0:2 * RW].rearrange("p (r w) -> p r w", r=2)
        gate_w = y_all[:, 12, 0:KD * NE].rearrange("p (k e) -> p k e", k=KD)
        eb_sb = y_all[:, 12, 64:64 + NE]
        r0 = y_all[:, 13, :]
        NBI = NE + 6
        biased = r0[:, 0:TB * NBI].rearrange("p (b e) -> p b e", b=TB)
        taken = r0[:, 256:256 + TB * NBI].rearrange("p (b e) -> p b e", b=TB)
        top8 = r0[:, 512:512 + TB * 8].rearrange("p (b e) -> p b e", b=TB)
        logit = r0[:, 640:640 + TB * NE].rearrange("p (b e) -> p b e", b=TB)
        ew = r0[:, 768:768 + TB * NE].rearrange("p (b e) -> p b e", b=TB)
        lmax = r0[:, 900:900 + TB]
        lsum = r0[:, 908:908 + TB]
        lrec = r0[:, 916:916 + TB]
        comb = y_all[:, 14, 0:ME * TB].rearrange("p (e b) -> p e b", e=ME)
        h_sb = y_all[:, 15, 0:2 * FF].rearrange("p (r f) -> p r f", r=2)
        sgu = y_all[:, 15, 2 * FF:4 * FF].rearrange("p (r f) -> p r f", r=2)
        ln_r = xs[:, 0:4, :].rearrange("p (r a) d -> p r (a d)", r=2)
        ln_s = sb("ln_s", [P, 2, 6])
        ln_m = sb("ln_m", [P, 2, 2])
        ln_v = sb("ln_v", [P, 2, 2])
        ids_sb = z_gate[:, 0, :].bitcast(I32)
        ge_b = z_gate[:, 1, :].bitcast(BF16)[:, 0:NT]
        hT_hi = sb("hT_hi", [FH, 2, 512], F32R)
        hT_lo = sb("hT_lo", [FH, 2, 512], F32R)

        names = ("ld_x ld_c z_const st_cum d_x d_dt a_dt s_dt s_dtT d_dtT "
                 "p_split u_done d_done s_done xt_done y_done ms_done "
                 "a_copy a_z a_silu a_decay a_sq a_ln a_rs "
                 "v_tap v_xs v_m v_yz v_y "
                 "ld_wo ld_late ln_st "
                 "p_mask v_xm h_done a_sg v_g v_gm "
                 "o0 o1 o2 r0 r1 r2 s0 s1 s2 l0 l1 l2 q0 q1 q2 n0 n1 n2 t0 t1 a_t0 a_t1 v_t1 "
                 "lg_done v_rt a_el v_comb p_ex gu_done a_sgu v_h ht_done a_hT v_hT dn_done st_out")
        S = {n: sem(n) for n in names.split()}
        ld_w = [sem("ld_w0"), sem("ld_w1")]
        ld_cum = [sem("ld_cum0"), sem("ld_cum1")]
        ld_ex = [sem("ld_ex0"), sem("ld_ex1")]
        block = ctx.enter_context(nc.Block())

        def ge(e, s, value):
            if not (isinstance(value, int) and value <= 0):
                e.wait_ge(s, value)

        def steps(e, step, after_first=None):
            step(0, 0, True, False)
            if after_first:
                after_first()
            step(1, 1, True, True)
            with e.Fori(0, (NPAIR - 2) // 2) as k:
                step(k * 2 + 2, 0, True, True)
                step(k * 2 + 3, 1, True, True)
            step(NPAIR, 0, False, True)

        def experts(e, step):
            step(0, 0, True)
            step(1, 1, False)
            with e.Fori(0, (ME - 3) // 2) as k:
                step(k * 2 + 2, 0, False)
                step(k * 2 + 3, 1, False)
            step(ME - 1, 0, False)

        cols = [(b * T, b * T + P) for b in range(NB)]

        @block.sync
        def _(sp):
            sp.dma_start(xT_raw, xT.rearrange("(k p) t -> p k t", p=P)).then_inc(S["ld_x"], 16)
            sp.dma_start(wdt, wdtT.rearrange("(k p) h -> p k h", p=P)).then_inc(S["ld_c"], 16)
            sp.dma_start(head_c[:, 0:1], dt_bias.rearrange("(h o) -> h o", o=1)).then_inc(S["ld_c"], 16)
            sp.dma_start(head_c[:, 1:2], a_log.rearrange("(h o) -> h o", o=1)).then_inc(S["ld_c"], 16)

            def load_pair(n, par):
                sp.dma_start(w_raw[:, par, :], winT[bass.ds(n, 1)].rearrange("a p w -> p (a w)")
                             ).then_inc(ld_w[par], 16)

            def load_cum(n, par):
                sp.dma_start(cum_l[3:6, par, :], cneg[:, bass.ds(2 * n, 2), :].rearrange("c h t -> c (h t)")
                             ).then_inc(ld_cum[par], 16)
                sp.dma_start(cum_r[0:3, par, :], cpos[:, bass.ds(2 * n, 2), :].rearrange("c h t -> c (h t)")
                             ).then_inc(ld_cum[par], 16)

            load_pair(0, 0)
            load_pair(1, 1)
            sp.wait_ge(S["d_dt"], 11)
            sp.dma_start(cpos.rearrange("c h t -> h c t"), cum_b[:, 0:3, :]).then_inc(S["st_cum"], 16)
            sp.dma_start(cneg.rearrange("c h t -> h c t"), cum_b[:, 3:6, :]).then_inc(S["st_cum"], 16)
            sp.wait_ge(S["st_cum"], 32)
            sp.wait_ge(S["z_const"], 3)
            load_cum(0, 0)
            load_cum(1, 1)
            with sp.Fori(0, (NPAIR - 2) // 2) as k:
                for par in range(2):
                    n = k * 2 + par
                    ge(sp, S["v_tap"], n * (6 * NCONV) + 6 * NCONV)
                    load_pair(n + 2, par)
                    ge(sp, S["d_done"], n * UNITS + UNITS)
                    load_cum(n + 2, par)

            sp.wait_ge(S["d_done"], NPAIR * UNITS)
            sp.dma_start(wo_sb, woutT.rearrange("(i p) d -> p i d", p=P)).then_inc(S["ld_wo"], 16)
            sp.wait_ge(S["v_m"], NPAIR * UNITS)
            sp.wait_ge(S["s_done"], NPAIR * UNITS)
            sp.wait_ge(S["v_xs"], 2 * NPAIR)
            sp.wait_ge(S["xt_done"], 2 * NPAIR)
            sp.wait_ge(S["v_yz"], 2 * NPAIR)
            sp.dma_start(x_tok, x.rearrange("(b p) d -> p b d", p=P)).then_inc(S["ld_late"], 16)
            sp.dma_start(ids_sb, ids.rearrange("(o t) -> o t", o=1).broadcast_to([P, NT])
                         ).then_inc(S["ld_late"], 16)
            sp.dma_start(ctx_w, ctxT.rearrange("e (k p) f -> p e k f", p=P)).then_inc(S["ld_late"], 16)
            sp.wait_ge(S["o0"], TB)
            sp.dma_start(gate_w, gateT.rearrange("(k p) e -> p k e", p=P)).then_inc(S["ld_late"], 16)
            sp.dma_start(eb_sb, ebias.rearrange("(o e) -> o e", o=1).broadcast_to([P, NE])
                         ).then_inc(S["ld_late"], 16)

            def load_expert(n, par):
                sp.dma_start(exp_raw[:, par, :], wexp[bass.ds(n, 1)].rearrange("a p w -> p (a w)")
                             ).then_inc(ld_ex[par], 16)
            load_expert(0, 0)
            load_expert(1, 1)

            def next_expert(n, par):
                ge(sp, S["p_ex"], n * 2 + 2)
                load_expert(n + 2, par)
            next_expert(0, 0)
            with sp.Fori(0, (ME - 3) // 2) as k:
                next_expert(k * 2 + 1, 1)
                next_expert(k * 2 + 2, 0)
            for b in range(TB):
                sp.wait_ge(S["n2"], b + 1)
                sp.dma_start(out[b * P:(b + 1) * P, :], x1[:, b, :]).then_inc(S["st_out"], 16)
            sp.wait_ge(S["st_out"], 16 * TB)

        @block.gpsimd
        def _(pool):
            made = [0]

            def link(ins):
                made[0] += 1
                ins.then_inc(S["z_const"], 1)
                pool.wait_ge(S["z_const"], made[0])

            link(pool.memset(cum_l, 1.0))
            link(pool.memset(zero[:, :], 0.0))
            link(pool.memset(cum_r, 1.0))
            link(pool.memset(ident[:, :], 0.0))
            link(pool.affine_select(out=ident[:, :], in_=ident[:, :], compare_op=ALU.not_equal, fill=1.0,
                                    base=0, pattern=[[-1, P]], channel_multiplier=1))
            link(pool.tensor_copy(ident_b[:, :], ident[:, :]))
            link(pool.memset(mask[:, :], 0.0))
            link(pool.affine_select(out=mask[:, 0:P], in_=mask[:, 0:P], compare_op=ALU.is_ge, fill=NEG,
                                    base=0, pattern=[[1, P]], channel_multiplier=-1))
            link(pool.affine_select(out=mask[:, T:SC], in_=mask[:, T:SC], compare_op=ALU.is_ge, fill=NEG,
                                    base=0, pattern=[[1, P]], channel_multiplier=-1))
            link(pool.memset(mean_w[:, :], 0.0))
            link(pool.memset(mean_w[0:HP, 0:HP], 1.0 / HP))
            link(pool.memset(mean_w[HP:P, HP:P], 1.0 / HP))
            link(pool.memset(eps_rms[:, :], RMS_EPS))
            link(pool.memset(eps_ln[:, :], LN_EPS))

            def split(n, par):
                pool.wait_ge(ld_w[par], n * 8 + (16 if par == 0 else 8))
                if not (isinstance(n, int) and n < 2):
                    ge(pool, S["u_done"], (n - 1) * 12)
                raw = w_raw[:, par, 0:KD * PW]
                pool.tensor_tensor(w_hi[:, par, :], raw, zero[:, :].broadcast_to([P, KD * PW]), ALU.add).then_inc(S["p_split"], 1)
                ge(pool, S["p_split"], n * 2 + 1)
                pool.tensor_tensor(w_lo[:, par, :], raw, w_hi[:, par, :].bitcast(F32), ALU.subtract
                                   ).then_inc(S["p_split"], 1)
            split(0, 0)
            split(1, 1)
            with pool.Fori(0, (NPAIR - 2) // 2) as k:
                split(k * 2 + 2, 0)
                split(k * 2 + 3, 1)

            pool.wait_ge(S["ld_late"], 48)
            mk = [0]

            def mlink(ins):
                mk[0] += 1
                ins.then_inc(S["p_mask"], 1)
                pool.wait_ge(S["p_mask"], mk[0])
            mlink(pool.tensor_scalar(emask[:, 0, :], ids_sb, float(TPE), None, ALU.is_lt))
            mlink(pool.tensor_scalar(emask[:, 1, :], ids_sb, float(TPE), None, ALU.is_ge))
            mlink(pool.tensor_scalar(ge_b, ids_sb, float(2 * TPE), None, ALU.is_ge))
            mlink(pool.tensor_scalar(emask[:, 3, :], ids_sb, float(3 * TPE), None, ALU.is_ge))
            mlink(pool.tensor_tensor(emask[:, 1, :], emask[:, 1, :], ge_b, ALU.subtract))
            mlink(pool.tensor_tensor(emask[:, 2, :], ge_b, emask[:, 3, :], ALU.subtract))

            def split_expert(n, par, first=False):
                pool.wait_ge(ld_ex[par], n * 8 + (16 if par == 0 else 8))
                if not (isinstance(n, int) and n < 2):
                    ge(pool, S["dn_done"], (n - 1) * TB)
                raw = exp_raw[:, par, :]
                pool.tensor_tensor(w_hi[:, par, 0:RW], raw, zero[:, :].broadcast_to([P, RW]), ALU.add).then_inc(S["p_ex"], 1)
                ge(pool, S["p_ex"], n * 2 + 1)
                pool.tensor_tensor(w_lo[:, par, 0:RW], raw, w_hi[:, par, 0:RW].bitcast(F32), ALU.subtract
                                   ).then_inc(S["p_ex"], 1)
            pool.wait_ge(S["u_done"], 12 * NPAIR)
            experts(pool, split_expert)

        @block.tensor
        def _(pe):
            pe.wait_ge(S["ld_x"], 16)
            pe.wait_ge(S["ld_c"], 48)
            for hf in range(2):
                for k in range(KD):
                    mm = pe.matmul(ps[0:H, hf, :], wdt[:, k, :], xT_raw[:, k, hf * 512:(hf + 1) * 512],
                                   start=(k == 0), stop=(k == KD - 1))
            mm.then_inc(S["s_dt"], 1)
            def turn_dt():
                pe.wait_ge(S["d_dt"], 2)
                pe.wait_ge(S["z_const"], 14)
                for b in range(TB):
                    mm = pe.transpose(ps[:, 4, b * H:(b + 1) * H], dt_l[:, b * P:(b + 1) * P], ident[0:H, 0:H])
                mm.then_inc(S["s_dtT"], 1)
                pe.wait_ge(S["d_dtT"], 1)

            def step(n, par, front, back):
                q, qp = n - 1, 1 - par
                if back:
                    pe.wait_ge(ld_cum[qp], q * 16 + (32 if qp == 0 else 16))
                for j in range(12):
                    k = j - 2
                    if back and j in (1, 2):
                        c = j - 1
                        ge(pe, S["a_silu"], q * NCONV + 1)
                        if c == 0:
                            ge(pe, S["a_ln"], q * 2)
                        else:
                            ge(pe, S["v_xs"], q * 2 + 1)
                        for b in range(4):
                            mm = pe.transpose(ps[:, 7, b * P:(b + 1) * P],
                                              conv[:, qp, 0, (4 * c + b) * P:(4 * c + b + 1) * P], ident[:, :])
                        mm.then_inc(S["xt_done"], 1)
                    if back and 0 <= k < UNITS:
                        b, h = k // 2, k % 2
                        c0, c1 = cols[b]
                        o = h * NT
                        ge(pe, S["a_decay"], q * UNITS + k)
                        pe.matmul(ps[:, 4, 0:SC], ident_b[:, :], mask[:, :], start=True, stop=False)
                        pe.matmul(ps[:, 4, 0:T], cum_l[:, qp, o + c0:o + c0 + P], cum_r[:, qp, o + c0:o + c0 + T],
                                  start=False, stop=False)
                        pe.matmul(ps[:, 4, T:SC], cum_l[:, qp, o + c1:o + c1 + P], cum_r[:, qp, o + c1:o + c1 + P],
                                  start=False, stop=True).then_inc(S["d_done"], 1)
                    if front:
                        if j == 0:
                            ge(pe, S["p_split"], n * 2 + 2)
                            if isinstance(n, int) and n == 0:
                                pe.wait_ge(S["d_x"], 3)
                        if j >= 4:
                            f, m = j - 4, n
                        else:
                            f, m = j + 8, n - 1
                        if not (isinstance(m, int) and m < 0):
                            if f < 2:
                                pe.wait_ge(S["a_z"], m * 2 + f + 1)
                            else:
                                ge(pe, S["v_tap"], m * (6 * NCONV) + 6 * (f // 2 - 1) + 5 + f % 2)
                        tile, hf = j // 2, j % 2
                        i = 0
                        for kk in range(KD):
                            w = slice(kk * PW + tile * P, kk * PW + tile * P + P)
                            t = slice(hf * 512, hf * 512 + 512)
                            for wp, xp in ((w_hi, x_hi), (w_hi, x_lo), (w_lo, x_hi)):
                                mm = pe.matmul(ps[:, j % 4, :], wp[:, par, w], xp[:, kk, t],
                                               start=(i == 0), stop=(i == 5))
                                i += 1
                        mm.then_inc(S["u_done"], 1)
                    if back and 0 <= k < UNITS:
                        b, h = k // 2, k % 2
                        c0, c1 = cols[b]
                        Bm, Cm = conv[:, qp, 1 + 2 * h, :], conv[:, qp, 2 + 2 * h, :]
                        ge(pe, S["a_silu"], q * NCONV + 3 + 2 * h)
                        ge(pe, S["v_m"], q * UNITS + k)
                        pe.matmul(ps[:, 5, 0:T], Bm[:, c0:c0 + P], Cm[:, c0:c0 + T], start=True, stop=True)
                        pe.matmul(ps[:, 5, T:SC], Bm[:, c1:c1 + P], Cm[:, c1:c1 + P], start=True, stop=True
                                  ).then_inc(S["s_done"], 1)
                    if back and 0 <= k - 1 < UNITS:
                        u = k - 1
                        b, h = u // 2, u % 2
                        y = ps[h * HP:(h + 1) * HP, 6, (b % 2) * T:(b % 2) * T + T]
                        ch = slice(h * HP, (h + 1) * HP)
                        ge(pe, S["v_xs"], q * 2 + 2)
                        ge(pe, S["v_m"], q * UNITS + u + 1)
                        if u % 4 == 0:
                            ge(pe, S["v_yz"], q * 2 + u // 4)
                            ge(pe, S["a_sq"], q * 2 + u // 4)
                        pe.matmul(y, xs[:, 2 * b, ch], scores[:, u % 2, 0:T], start=True, stop=False,
                                  skip_group_check=True)
                        mm = pe.matmul(y[:, P:T], xs[:, 2 * b + 1, ch], scores[:, u % 2, T:SC], start=False,
                                       stop=True, skip_group_check=True)
                        mm.then_inc(S["y_done"], 1)
                    if back and j in (8, 11):
                        g = 0 if j == 8 else 1
                        ge(pe, S["a_sq"], q * 2 + g + 1)
                        ge(pe, S["v_xs"], q * 2 + 2)
                        ge(pe, S["a_ln"], q * 2 + g)
                        pe.matmul(ps[:, 7, :], mean_w[:, :], y_sq[:, :], start=True, stop=True
                                  ).then_inc(S["ms_done"], 1)

            steps(pe, step, turn_dt)

            def turn(b, n_sem, a_sem, t_sem, src, bank):
                pe.wait_ge(n_sem, b + 1)
                if b >= 2:
                    pe.wait_ge(a_sem, b - 1)
                for k in range(KD):
                    mm = pe.transpose(ps[:, bank + b % 2, k * P:(k + 1) * P], src[:, b, k * P:(k + 1) * P],
                                      ident[:, :])
                mm.then_inc(t_sem, 1)

            pe.wait_ge(S["v_y"], 2 * NPAIR)
            pe.wait_ge(S["ld_wo"], 16)
            for b in range(TB):
                if b >= 2:
                    ge(pe, S["r0"], b - 1)
                for i in range(NPAIR):
                    mm = pe.matmul(ps[:, b % 2, 0:D], y_all[:, i, b * P:(b + 1) * P], wo_sb[:, i, :],
                                   start=(i == 0), stop=(i == NPAIR - 1))
                mm.then_inc(S["o0"], 1)
                if b >= 1:
                    turn(b - 1, S["n0"], S["a_t0"], S["t0"], x1, 2)
            turn(TB - 1, S["n0"], S["a_t0"], S["t0"], x1, 2)

            pe.wait_ge(S["ld_late"], 48)
            for hf in range(2):
                if hf:
                    pe.wait_ge(S["v_g"], 1)
                for e in range(EX):
                    pe.wait_ge(S["v_xm"], hf * EX + e + 1)
                    for m in range(2):
                        for k in range(KD):
                            mm = pe.matmul(ps[:, 4 + m, :], ctx_w[:, e, k, m * P:(m + 1) * P], xm[:, e % 2, k, :],
                                           start=(e == 0 and k == 0), stop=(e == EX - 1 and k == KD - 1))
                    mm.then_inc(S["h_done"], 1)
                for b in range(4 * hf, 4 * hf + 4):
                    if b >= 2:
                        ge(pe, S["r1"], b - 1)
                    pe.wait_ge(S["v_gm"], hf * EX + EX)
                    for e in range(EX):
                        for k in range(KD):
                            mm = pe.matmul(ps[:, b % 2, 0:D], gm[:, e, k, (b % 4) * P:(b % 4) * P + P],
                                           ctx_w[:, e, k, :], start=(e == 0 and k == 0),
                                           stop=(e == EX - 1 and k == KD - 1))
                    mm.then_inc(S["o1"], 1)
                    if b >= 1:
                        turn(b - 1, S["n1"], S["a_t1"], S["t1"], x2, 2)
            turn(TB - 1, S["n1"], S["a_t1"], S["t1"], x2, 2)

            pe.wait_ge(S["a_t1"], TB)
            pe.wait_ge(S["ld_late"], 80)
            pe.wait_ge(S["r1"], TB)
            for b in range(TB):
                for k in range(KD):
                    mm = pe.matmul(ps[:, 0, b * NE:(b + 1) * NE], x2T[:, k, b * P:(b + 1) * P], gate_w[:, k, :],
                                   start=(k == 0), stop=(k == KD - 1))
            mm.then_inc(S["lg_done"], 1)
            pe.wait_ge(S["v_rt"], 2)
            pe.wait_ge(S["v_t1"], 2)

            def down(n, par, first, b):
                ge(pe, S["v_hT"], n * 4 + b // 2 + 1)
                for k in range(2):
                    hs = slice(((b % 2) * 2 + k) * P, ((b % 2) * 2 + k + 1) * P)
                    ws = slice(KD * 2 * FF + k * D, KD * 2 * FF + (k + 1) * D)
                    for i, (hp, wp) in enumerate(((hT_hi, w_hi), (hT_hi, w_lo), (hT_lo, w_hi))):
                        mm = pe.matmul(ps[:, 4 + b // 2, (b % 2) * D:(b % 2) * D + D], hp[:, (b // 2) % 2, hs],
                                       wp[0:FH, par, ws], start=(first and b % 2 == 0 and k == 0 and i == 0),
                                       stop=False, skip_group_check=True)
                mm.then_inc(S["dn_done"], 1)

            def turn_h(n, b):
                ge(pe, S["v_h"], n * TB + b + 1)
                if b % 2 == 0:
                    ge(pe, S["v_hT"], n * 4 + b // 2 - 1)
                for k in range(2):
                    c = ((b % 2) * 2 + k) * P
                    mm = pe.transpose(ps[0:FH, 2 + (b // 2) % 2, c:c + P], h_sb[:, b % 2, k * FH:(k + 1) * FH],
                                      ident[:, :])
                mm.then_inc(S["ht_done"], 1)

            def expert(n, par, first):
                ge(pe, S["p_ex"], n * 2 + 2)
                for b in range(TB):
                    if not (first and b < 2):
                        ge(pe, S["v_h"], n * TB + b - 1)
                    i = 0
                    for k in range(KD):
                        w = slice(k * 2 * FF, (k + 1) * 2 * FF)
                        for xp, wp in ((x_hi, w_hi), (x_hi, w_lo), (x_lo, w_hi)):
                            mm = pe.matmul(ps[:, b % 2, 0:2 * FF], xp[:, k, b * P:(b + 1) * P], wp[:, par, w],
                                           start=(i == 0), stop=(i == 5))
                            i += 1
                    mm.then_inc(S["gu_done"], 1)
                    if b >= 1:
                        turn_h(n, b - 1)
                    elif not first:
                        turn_h(n - 1, TB - 1)
                    if b >= 4:
                        down(n, par, first, b - 4)
                    elif not first:
                        down(n - 1, 1 - par, isinstance(n, int) and n == 1, b + 4)

            experts(pe, expert)
            turn_h(ME - 1, TB - 1)
            for b in range(4, TB):
                down(ME - 1, 0, False, b)

        @block.scalar
        def _(act):
            act.wait_ge(S["z_const"], 14)
            act.preload_act_table_set("natural_log_exp_and_others")
            act.wait_ge(S["ld_c"], 48)
            act.activation(head_c[:, 2:3], head_c[:, 1:2], ACT.Exp).then_inc(S["a_dt"], 1)
            act.wait_ge(S["a_dt"], 1)
            act.wait_ge(S["d_x"], 4)
            act.activation(dt_e, dt_e, ACT.Exp, scale=-1.0).then_inc(S["a_dt"], 1)
            act.wait_ge(S["a_dt"], 2)
            act.activation(dt_ch, dt_e, ACT.Ln, bias=1.0).then_inc(S["a_dt"], 1)

            def step(n, par, front, back):
                q, qp = n - 1, 1 - par

                def silu(tile):
                    ge(act, S["v_tap"], q * (6 * NCONV) + 6 * (tile + 1))
                    act.activation(conv[:, qp, tile, :], conv[:, qp, tile, :], ACT.Silu).then_inc(S["a_silu"], 1)

                def z(hf):
                    ge(act, S["u_done"], n * 12 + hf + 1)
                    if not (isinstance(n, int) and n < 2):
                        ge(act, S["v_yz"], n * 2 - 2)
                    act.activation(z_gate[:, par, hf * 512:(hf + 1) * 512], ps[:, hf, :], ACT.Silu
                                   ).then_inc(S["a_z"], 1)

                def copy(j):
                    tile, hf = j // 2 - 1, j % 2
                    ge(act, S["u_done"], n * 12 + j + 1)
                    if j == 2 and not (isinstance(n, int) and n < 2):
                        ge(act, S["s_done"], n * UNITS - UNITS)
                    tap = KD * PW + tile * TAPS + TAPS - 1
                    act.activation(conv[:, par, tile, hf * 512:(hf + 1) * 512], ps[:, j % 4, :], ACT.Copy,
                                   scale=w_raw[:, par, tap:tap + 1]).then_inc(S["a_copy"], 1)

                def exp_decay(k):
                    ge(act, S["d_done"], q * UNITS + k + 1)
                    ge(act, S["v_m"], q * UNITS + max(k - 1, 0))
                    act.activation(decay[:, k % 2, :], ps[:, 4, 0:SC], ACT.Exp).then_inc(S["a_decay"], 1)

                def square(g):
                    ge(act, S["y_done"], q * UNITS + 4 * g + 4)
                    ge(act, S["ms_done"], q * 2 + g)
                    act.activation(y_sq[:, :], ps[:, 6, :], ACT.Square).then_inc(S["a_sq"], 1)

                def rsqrt(g):
                    ge(act, S["ms_done"], q * 2 + g + 1)
                    ge(act, S["v_y"], q * 2 + g)
                    act.activation(y_rs[:, :], ps[:, 7, :], ACT.Ln, bias=eps_rms[:, 0:1]).then_inc(S["a_ln"], 1)
                    ge(act, S["a_ln"], q * 2 + g + 1)
                    act.activation(y_rs[:, :], y_rs[:, :], ACT.Exp, scale=-0.5).then_inc(S["a_rs"], 1)

                act.preload_act_table_set("silu_and_others")
                if back:
                    silu(0)
                if front:
                    z(0)
                if back:
                    silu(1)
                    silu(2)
                if front:
                    z(1)
                    copy(2)
                if back:
                    silu(3)
                    silu(4)
                    act.preload_act_table_set("natural_log_exp_and_others")
                    exp_decay(0)
                for j in range(3, 12):
                    if back and j == 7:
                        square(0)
                    if front:
                        copy(j)
                    if back and j - 2 < UNITS:
                        exp_decay(j - 2)
                    if back and j == 9:
                        rsqrt(0)
                if back:
                    square(1)
                    rsqrt(1)

            steps(act, step)

            def layer_norm_scale(b, i):
                act.wait_ge(S[f"s{i}"], b + 1)
                act.activation(ln_v[:, b % 2, 0:1], ln_m[:, b % 2, 1:2], ACT.Ln, bias=eps_ln[:, 0:1]
                               ).then_inc(S[f"l{i}"], 1)
                act.wait_ge(S[f"l{i}"], b + 1)
                act.activation(ln_v[:, b % 2, 1:2], ln_v[:, b % 2, 0:1], ACT.Exp, scale=-0.5
                               ).then_inc(S[f"q{i}"], 1)

            def take_turned(b, t_sem, a_sem, dst):
                act.wait_ge(t_sem, b + 1)
                act.activation(dst[:, :, b * P:(b + 1) * P],
                               ps[:, 2 + b % 2, 0:D].rearrange("p (k t) -> p k t", k=KD), ACT.Copy
                               ).then_inc(a_sem, 1)

            for b in range(TB):
                layer_norm_scale(b, 0)
                if b >= 1:
                    take_turned(b - 1, S["t0"], S["a_t0"], x1T)
            take_turned(TB - 1, S["t0"], S["a_t0"], x1T)

            for hf in range(2):
                act.preload_act_table_set("silu_and_others")
                act.wait_ge(S["h_done"], hf * EX + EX)
                act.activation(sg_sb[:, :, :], ps[:, 4:6, :], ACT.Silu).then_inc(S["a_sg"], 1)
                act.preload_act_table_set("natural_log_exp_and_others")
                for b in range(4 * hf, 4 * hf + 4):
                    layer_norm_scale(b, 1)
                    if b >= 1:
                        take_turned(b - 1, S["t1"], S["a_t1"], x2T)
            take_turned(TB - 1, S["t1"], S["a_t1"], x2T)

            act.wait_ge(S["v_rt"], 4)
            act.activation(ew, ew, ACT.Exp).then_inc(S["a_el"], 1)

            act.preload_act_table_set("silu_and_others")

            def expert(n, par, first):
                def take_h(m, c):
                    act.wait_ge(S["ht_done"], m * TB + 2 * c + 2)
                    if not (isinstance(m, int) and m == 0 and c < 2):
                        act.wait_ge(S["dn_done"], m * TB + 2 * c - 2)
                    act.activation(hT_hi[:, c % 2, :], ps[0:FH, 2 + c % 2, :], ACT.Copy).then_inc(S["a_hT"], 1)
                for b in range(TB):
                    ge(act, S["gu_done"], n * TB + b + 1)
                    if not (first and b < 2):
                        ge(act, S["v_h"], n * TB + b - 1)
                    act.activation(sgu[:, b % 2, :], ps[:, b % 2, 0:FF], ACT.Silu).then_inc(S["a_sgu"], 1)
                    if b in (2, 4, 6):
                        take_h(n, b // 2 - 1)
                    if b == 0 and not first:
                        take_h(n - 1, 3)
            experts(act, expert)
            act.wait_ge(S["ht_done"], ME * TB)
            act.wait_ge(S["dn_done"], ME * TB - 4)
            act.activation(hT_hi[:, 1, :], ps[0:FH, 3, :], ACT.Copy).then_inc(S["a_hT"], 1)

            act.preload_act_table_set("natural_log_exp_and_others")
            for b in range(TB):
                layer_norm_scale(b, 2)

        @block.vector
        def _(dve):
            dve.wait_ge(S["ld_x"], 16)
            dve.tensor_copy(x_hi[:, :, :], xT_raw).then_inc(S["d_x"], 1)
            dve.wait_ge(S["d_x"], 1)
            dve.tensor_tensor(x_lo[:, :, :], xT_raw, x_hi[:, :, :].bitcast(F32), ALU.subtract).then_inc(S["d_x"], 1)
            dve.wait_ge(S["ld_c"], 48)
            dve.wait_ge(S["s_dt"], 1)
            dve.tensor_scalar(dt_z, ps[0:H, 0:2, :].rearrange("p a t -> p (a t)"), head_c[:, 0:1], None, ALU.add
                              ).then_inc(S["d_x"], 1)
            dve.wait_ge(S["d_x"], 3)
            dve.scalar_tensor_tensor(out=dt_e, in0=dt_z, scalar=-1.0, in1=dt_z, op0=ALU.mult, op1=ALU.max).then_inc(S["d_x"], 1)
            made = [0]

            def link(ins):
                made[0] += 1
                ins.then_inc(S["d_dt"], 1)
                dve.wait_ge(S["d_dt"], made[0])
            link(dve.tensor_scalar(dt_l, dt_z, 0.0, None, ALU.max))
            def run_dt():
                dve.wait_ge(S["a_dt"], 3)
                link(dve.tensor_tensor(dt_l, dt_l, dt_ch, ALU.add))
                link(dve.tensor_scalar(dt_da, dt_l, head_c[:, 2:3], -1.0, ALU.mult, ALU.mult))
                link(dve.memset(dt_z, 1.0))
                for b in range(NB):
                    t = slice(b * T, (b + 1) * T)
                    ins = dve.tensor_tensor_scan(dt_cum[:, t], dt_z[:, t], dt_da[:, t], 0.0, ALU.mult, ALU.add)
                link(ins)
                link(dve.tensor_copy(cum_b[:, 0, :], dt_cum))
                link(dve.tensor_tensor(dt_r, dt_cum, cum_b[:, 0, :], ALU.subtract))
                link(dve.tensor_copy(cum_b[:, 1, :], dt_r))
                link(dve.tensor_tensor(dt_cum, dt_r, cum_b[:, 1, :], ALU.subtract))
                link(dve.tensor_copy(cum_b[:, 2, :], dt_cum))
                link(dve.tensor_scalar(cum_b[:, 3:6, :], cum_b[:, 0:3, :], -1.0, None, ALU.mult))
                dve.wait_ge(S["s_dtT"], 1)
                link(dve.tensor_copy(dt_tok[:, :, :], ps[:, 4, 0:TB * H].rearrange("p (b h) -> p b h", b=TB)))
                dve.sem_inc(S["d_dtT"], 1)
                dve.wait_ge(S["st_cum"], 32)

            def step(n, par, front, back):
                q, qp = n - 1, 1 - par

                def x_scaled(c):
                    ge(dve, S["xt_done"], q * 2 + c + 1)
                    if c == 0 and not (isinstance(q, int) and q == 0):
                        ge(dve, S["y_done"], q * UNITS)
                    dve.tensor_tensor(xs[:, 4 * c:4 * c + 4, :].rearrange("p b (h c) -> p b h c", h=2),
                                      ps[:, 7, :].rearrange("p (b h c) -> p b h c", b=4, h=2),
                                      dt_tok[:, 4 * c:4 * c + 4, bass.ds(q * 2, 2)].unsqueeze(3)
                                      .broadcast_to([P, 4, 2, HP]), ALU.mult).then_inc(S["v_xs"], 1)

                def weigh(k):
                    ge(dve, S["a_decay"], q * UNITS + k + 1)
                    ge(dve, S["s_done"], q * UNITS + k + 1)
                    ge(dve, S["y_done"], q * UNITS + max(k - 1, 0))
                    dve.tensor_tensor(scores[:, k % 2, :], ps[:, 5, 0:SC], decay[:, k % 2, :], ALU.mult
                                      ).then_inc(S["v_m"], 1)

                def tap(m, s, hf):
                    j = 2 * (m + 1) + hf
                    if s == 1:
                        ge(dve, S["a_copy"], n * (2 * NCONV) + 2 * m + hf + 1)
                    else:
                        ge(dve, S["v_tap"], n * (6 * NCONV) + 6 * m + 2 * (s - 2) + hf + 1)
                    o = conv[:, par, m, hf * 512:(hf + 1) * 512].rearrange("p (b t) -> p b t", b=2)
                    u = ps[:, j % 4, :].rearrange("p (b t) -> p b t", b=2)
                    c = KD * PW + m * TAPS + TAPS - 1 - s
                    dve.scalar_tensor_tensor(out=o[:, :, s:], in0=u[:, :, 0:T - s],
                                             scalar=w_raw[:, par, c:c + 1], in1=o[:, :, s:],
                                             op0=ALU.mult, op1=ALU.add).then_inc(S["v_tap"], 1)

                def gate(g):
                    ge(dve, S["y_done"], q * UNITS + 4 * g + 4)
                    ge(dve, S["a_z"], q * 2 + g + 1)
                    ge(dve, S["a_sq"], q * 2 + g + 1)
                    ge(dve, S["v_y"], q * 2 + g)
                    dve.tensor_tensor(y_gated[:, :], ps[:, 6, :], z_gate[:, qp, g * 512:(g + 1) * 512], ALU.mult
                                      ).then_inc(S["v_yz"], 1)

                def norm(g):
                    ge(dve, S["a_rs"], q * 2 + g + 1)
                    ge(dve, S["v_yz"], q * 2 + g + 1)
                    dst = y_all[:, bass.ds(q, 1), g * 512:(g + 1) * 512].rearrange("p a t -> p (a t)")
                    dve.tensor_tensor(dst, y_gated[:, :], y_rs[:, :], ALU.mult).then_inc(S["v_y"], 1)

                if back:
                    x_scaled(0)
                    x_scaled(1)
                for m in range(NCONV):
                    if back and m < 4:
                        weigh(2 * m)
                    if back and m == 4:
                        norm(0)
                    if front:
                        tap(m, 1, 0)
                        tap(m, 1, 1)
                        tap(m, 2, 0)
                    if back and m == 2:
                        gate(0)
                    if back and m < 4:
                        weigh(2 * m + 1)
                    if front:
                        tap(m, 2, 1)
                        tap(m, 3, 0)
                        tap(m, 3, 1)
                if back:
                    gate(1)
                    norm(1)

            steps(dve, step, run_dt)

            def layer_norm(b, i, src, res, dst):
                r = ln_r[:, b % 2, :]
                if i < 2:
                    dve.wait_ge(S[f"o{i}"], b + 1)
                dve.tensor_tensor(r, src, res, ALU.add).then_inc(S[f"r{i}"], 1)
                dve.wait_ge(S[f"r{i}"], b + 1)
                stat(dve.bn_stats(ln_s[:, b % 2, :], r))
                dve.bn_aggr(ln_m[:, b % 2, :], ln_s[:, b % 2, :]).then_inc(S[f"s{i}"], 1)
                dve.wait_ge(S[f"q{i}"], b + 1)
                dve.wait_ge(S[f"s{i}"], b + 1)
                dve.tensor_scalar(dst, r, ln_m[:, b % 2, 0:1], ln_v[:, b % 2, 1:2], ALU.subtract, ALU.mult
                                  ).then_inc(S[f"n{i}"], 1)
            stats = [0]

            def stat(ins):
                stats[0] += 1
                ins.then_inc(S["ln_st"], 1)
                dve.wait_ge(S["ln_st"], stats[0])

            dve.wait_ge(S["ld_late"], 48)
            for b in range(TB):
                layer_norm(b, 0, ps[:, b % 2, 0:D], x_tok[:, b, :], x1[:, b, :])

            dve.wait_ge(S["p_mask"], 6)
            dve.wait_ge(S["a_t0"], TB)
            for hf in range(2):
                t = slice(hf * 512, (hf + 1) * 512)
                for e in range(EX):
                    if hf * EX + e >= 2:
                        ge(dve, S["h_done"], hf * EX + e - 1)
                    dve.tensor_tensor(xm[:, e % 2, :, :], x1T[:, :, t],
                                      emask[:, e, t].unsqueeze(1).broadcast_to([P, KD, 512]), ALU.mult
                                      ).then_inc(S["v_xm"], 1)
                dve.wait_ge(S["a_sg"], hf + 1)
                dve.tensor_tensor(g_sb, sg_sb, ps[:, 4:6, :], ALU.mult).then_inc(S["v_g"], 1)
                dve.wait_ge(S["v_g"], hf + 1)
                if hf:
                    dve.wait_ge(S["o1"], 4)
                for e in range(EX):
                    dve.tensor_tensor(gm[:, e, :, :], g_sb,
                                      emask[:, e, t].unsqueeze(1).broadcast_to([P, KD, 512]), ALU.mult
                                      ).then_inc(S["v_gm"], 1)
                for b in range(4 * hf, 4 * hf + 4):
                    layer_norm(b, 1, ps[:, b % 2, 0:D], x1[:, b, :], x2[:, b, :])

            dve.wait_ge(S["a_t1"], TB)
            dve.tensor_copy(x_hi[:, :, :], x2T).then_inc(S["v_t1"], 1)
            dve.wait_ge(S["v_t1"], 1)
            dve.tensor_tensor(x_lo[:, :, :], x2T, x_hi[:, :, :].bitcast(F32), ALU.subtract).then_inc(S["v_t1"], 1)

            made[0] = 0

            def rlink(ins):
                made[0] += 1
                ins.then_inc(S["v_rt"], 1)
                dve.wait_ge(S["v_rt"], made[0])
            dve.wait_ge(S["lg_done"], 1)
            dve.wait_ge(S["ld_late"], 80)
            lg = ps[:, 0, 0:TB * NE].rearrange("p (b e) -> p b e", b=TB)
            rlink(dve.tensor_copy(logit, lg))
            rlink(dve.tensor_tensor(biased[:, :, 0:NE], lg, eb_sb.unsqueeze(1).broadcast_to([P, TB, NE]), ALU.add))
            rlink(dve.tensor_reduce(lmax, logit, AX.X, ALU.max))
            rlink(dve.tensor_tensor(ew, logit, lmax.unsqueeze(2).broadcast_to([P, TB, NE]), ALU.subtract))
            rlink(dve.memset(biased[:, :, NE:NBI], PAD))
            for b in range(TB):
                ins = dve.max(top8[:, b, :], biased[:, b, 0:NE])
            rlink(ins)
            rlink(dve.memset(top8[:, :, 2:8], PAD))
            for b in range(TB):
                ins = dve.match_replace(out=taken[:, b, :], in_to_replace=top8[:, b, :], in_values=biased[:, b, :],
                                        imm_value=HIT)
            rlink(ins)
            rlink(dve.tensor_tensor(taken[:, :, 0:NE], taken[:, :, 0:NE], biased[:, :, 0:NE], ALU.not_equal))
            dve.wait_ge(S["a_el"], 1)
            rlink(dve.tensor_tensor(ew, ew, taken[:, :, 0:NE], ALU.mult))
            rlink(dve.tensor_reduce(lsum, ew, AX.X, ALU.add))
            rlink(dve.reciprocal(lrec, lsum))
            rlink(dve.memset(comb[:, NE, :], 1.0))
            rlink(dve.tensor_tensor(comb[:, 0:NE, :].rearrange("p e b -> p b e"), ew,
                                    lrec.unsqueeze(2).broadcast_to([P, TB, NE]), ALU.mult))

            def expert(n, par, first):
                def take_h(m, c):
                    dve.wait_ge(S["a_hT"], m * 4 + c + 1)
                    dve.tensor_tensor(hT_lo[:, c % 2, :], ps[0:FH, 2 + c % 2, :], hT_hi[:, c % 2, :].bitcast(F32),
                                      ALU.subtract).then_inc(S["v_hT"], 1)
                for b in range(TB):
                    ge(dve, S["a_sgu"], n * TB + b + 1)
                    if not (first and b < 2):
                        ge(dve, S["ht_done"], n * TB + b - 1)
                    dve.scalar_tensor_tensor(out=h_sb[:, b % 2, :], in0=sgu[:, b % 2, :],
                                             scalar=comb[:, bass.ds(n, 1), b:b + 1].rearrange("p a b -> p (a b)"),
                                             in1=ps[:, b % 2, FF:2 * FF], op0=ALU.mult, op1=ALU.mult
                                             ).then_inc(S["v_h"], 1)
                    if b in (2, 4, 6):
                        take_h(n, b // 2 - 1)
                    if b == 0 and not first:
                        take_h(n - 1, 3)
            experts(dve, expert)
            dve.wait_ge(S["a_hT"], ME * 4)
            dve.tensor_tensor(hT_lo[:, 1, :], ps[0:FH, 3, :], hT_hi[:, 1, :].bitcast(F32), ALU.subtract
                              ).then_inc(S["v_hT"], 1)
            dve.wait_ge(S["dn_done"], ME * TB)
            for b in range(TB):
                layer_norm(b, 2, ps[:, 4 + b // 2, (b % 2) * D:(b % 2) * D + D], x2[:, b, :], x1[:, b, :])


_OUT = (NB, T, D)


def kernel(**inputs):
    import numpy as np
    import concourse.bacc as bacc
    from concourse.bass_utils import run_bass_kernel_spmd

    g = {k: np.asarray(v) for k, v in inputs.items()}
    x = g["x"].reshape(NT, D)
    win = g["L0_attn_Win"]
    o_z, o_b, o_c, o_dt = H * HP, 2 * H * HP, 2 * H * HP + H * N, 2 * H * HP + 2 * H * N

    def rows(i):
        t = [win[o_z + P * i:][:P], win[P * i:][:P]]
        for h in (2 * i, 2 * i + 1):
            t += [win[o_b + N * h:][:N], win[o_c + N * h:][:N]]
        return np.concatenate(t, 0)
    cx = g["L0_attn_conv_w_x"].reshape(NPAIR, P, TAPS)
    cb, cc = g["L0_attn_conv_w_b"], g["L0_attn_conv_w_c"]
    pairs = []
    for i in range(NPAIR):
        w = rows(i).T.reshape(KD, P, PW).transpose(1, 0, 2).reshape(P, KD * PW)
        taps = [cx[i], cb[2 * i], cc[2 * i], cb[2 * i + 1], cc[2 * i + 1]]
        pairs.append(np.concatenate([w] + taps, 1))
    wg = np.concatenate([g["L0_ffn_w_gate"], g["L0_ffn_sw_gate"][None]], 0)
    wu = np.concatenate([g["L0_ffn_w_up"], g["L0_ffn_sw_up"][None]], 0)
    wd = np.concatenate([g["L0_ffn_w_down"], g["L0_ffn_sw_down"][None]], 0)
    gu = np.concatenate([wg, wu], 1).transpose(0, 2, 1).reshape(ME, KD, P, 2 * FF)
    gu = gu.transpose(0, 2, 1, 3).reshape(ME, P, KD * 2 * FF)
    dn = np.zeros((ME, P, 2 * D), wd.dtype)
    dn[:, :FH] = wd.transpose(0, 2, 1).reshape(ME, 2, FH, D).transpose(0, 2, 1, 3).reshape(ME, FH, 2 * D)
    arrays = {
        "xT": x.T, "x": x, "winT": np.stack(pairs), "wdtT": win[o_dt:].T,
        "a_log": g["L0_attn_A_log"], "dt_bias": g["L0_attn_dt_bias"], "woutT": g["L0_attn_Wout"].T,
        "ids": g["itok_BxS_13_99985"].reshape(NT), "ctxT": g["ctx_2048"].transpose(0, 2, 1),
        "gateT": g["L0_ffn_gate_w"].T, "ebias": g["L0_ffn_expert_bias"],
        "wexp": np.concatenate([gu, dn], 2),
    }
    arrays = {f"in_{k}": np.ascontiguousarray(v) for k, v in arrays.items()}
    nc = bacc.Bacc("TRN2", target_bir_lowering=False, num_devices=1)
    args = [nc.dram_tensor(n, a.shape, mybir.dt.from_np(a.dtype), kind="ExternalInput").ap()
            for n, a in arrays.items()]
    out = nc.dram_tensor("out", (NT, D), F32, kind="ExternalOutput").ap()
    build_layer(nc, *args, out)
    r = run_bass_kernel_spmd(nc, [arrays], core_ids=[0])
    return r.results[0]["out"].reshape(_OUT)
```

```python
import concourse.bass as bass
from concourse import mybir
from contextlib import ExitStack

F32 = mybir.dt.float32
F32R = mybir.dt.float32r
BF16 = mybir.dt.bfloat16
I32 = mybir.dt.int32
ALU = mybir.AluOpType
ACT = mybir.ActivationFunctionType
AX = mybir.AxisListType

P = 128
NB, T, D = 4, 256, 256
NT = NB * T
TB = NT // P
KD = D // P
H, HP, N, TAPS = 32, 64, 128, 4
NPAIR = H // 2
NTILE = 6
NCONV = NTILE - 1
PW = NTILE * P
RAWW = KD * PW + NCONV * TAPS
TAP_N = 4 * NCONV
UNITS = 2 * NB
SC = T + P
EX = 4
VOCAB = 12500
TPE = VOCAB // EX
NE, FF = 16, 176
FH = FF // 2
ME = NE + 1
RW = KD * 2 * FF + 2 * D
NEG = -1.0e30
PAD = -3.0e38
HIT = 3.0e38
LN_EPS = 1e-5
RMS_EPS = 1e-6


def build_layer(nc, xT, x, winT, wdtT, a_log, dt_bias, woutT, ids, ctxT, gateT, ebias, wexp, out):
    cum_dram = nc.dram_tensor("cum_scratch", (H, NT), F32, kind="Internal").ap()

    with ExitStack() as ctx:
        def sb(name, shape, dt=F32):
            return ctx.enter_context(nc.sbuf_tensor(name, shape, dt))

        def sem(name):
            return ctx.enter_context(nc.semaphore(name))

        ps = ctx.enter_context(nc.psum_tensor("ps", [P, 8, 512], F32))

        x_hi = sb("x_hi", [P, KD, NT], F32R)
        x_lo = sb("x_lo", [P, KD, NT], F32R)
        w_raw = sb("w_raw", [P, 2, RAWW])
        w_hi = sb("w_hi", [P, 2, KD * PW], F32R)
        w_lo = sb("w_lo", [P, 2, KD * PW], F32R)
        conv = sb("conv", [P, 2, NCONV, NT])
        z_gate = sb("z_gate", [P, 2, NT])
        xs = sb("xs", [P, TB, P])
        decay = sb("decay", [P, 4, SC])
        scores = sb("scores", [P, 2, SC])
        y_all = sb("y_all", [P, NPAIR, NT])
        y_sq = sb("y_sq", [P, 512])
        y_rs = sb("y_rs", [P, 2, 512])
        cum_b = sb("cum_b", [P, 2, 2, NT])
        dt_tok = sb("dt_tok", [P, TB, H])
        cum_tok = sb("cum_tok", [P, TB, H])
        ident = sb("ident", [P, P])
        mean_w = sb("mean_w", [P, P])
        mask = sb("mask", [P, P])
        eps_rms = sb("eps_rms", [P, 1])
        eps_ln = sb("eps_ln", [P, 1])
        zero = sb("zero", [P, 1])
        head_c = sb("head_c", [H, 3])

        xT_raw = y_all[:, 0:2, :]
        wdt = y_all[:, 2, 0:KD * H].rearrange("p (k h) -> p k h", k=KD)
        dt_z, dt_e, dt_l, dt_ch, dt_da, dt_cum = (y_all[0:H, 3 + i, :] for i in range(6))

        conv_f = conv[:, :, :, :].rearrange("p a b t -> p (a b t)")
        at = [0]

        def carve(n):
            at[0] += n
            return conv_f[:, at[0] - n:at[0]]
        x_tok = carve(TB * D).rearrange("p (b d) -> p b d", b=TB)
        x1 = carve(TB * D).rearrange("p (b d) -> p b d", b=TB)
        x2 = x_tok
        x1T = carve(KD * NT).rearrange("p (k t) -> p k t", k=KD)
        ctx_w = carve(EX * KD * D).rearrange("p (e k f) -> p e k f", e=EX, k=KD)
        xm = w_raw[:, :, 0:KD * 512].rearrange("p r (k t) -> p r k t", k=KD)
        emask = carve(EX * NT // 2).bitcast(BF16).rearrange("p (e t) -> p e t", e=EX)
        wo_sb = cum_b[:, :, :, :].rearrange("p a b t -> p (a b t)").rearrange("p (i d) -> p i d", i=NPAIR)
        gm = y_all[:, 0:4, :].rearrange("p e (k t) -> p e k t", k=KD)
        g_sb = y_all[:, 4, :].rearrange("p (k t) -> p k t", k=KD)
        sg_sb = y_all[:, 5, :].rearrange("p (k t) -> p k t", k=KD)
        x2T = y_all[:, 6:8, :]
        exp_raw = y_all[:, 8:12, :].rearrange("p a t -> p (a t)")[:, 0:2 * RW].rearrange("p (r w) -> p r w", r=2)
        gate_w = y_all[:, 12, 0:KD * NE].rearrange("p (k e) -> p k e", k=KD)
        eb_sb = y_all[:, 12, 64:64 + NE]
        r0 = y_all[:, 13, :]
        NBI = NE + 6
        biased = r0[:, 0:TB * NBI].rearrange("p (b e) -> p b e", b=TB)
        taken = r0[:, 256:256 + TB * NBI].rearrange("p (b e) -> p b e", b=TB)
        top8 = r0[:, 512:512 + TB * 8].rearrange("p (b e) -> p b e", b=TB)
        logit = r0[:, 640:640 + TB * NE].rearrange("p (b e) -> p b e", b=TB)
        ew = r0[:, 768:768 + TB * NE].rearrange("p (b e) -> p b e", b=TB)
        lmax = r0[:, 900:900 + TB]
        lsum = r0[:, 908:908 + TB]
        lrec = r0[:, 916:916 + TB]
        comb = y_all[:, 14, 0:ME * TB].rearrange("p (e b) -> p e b", e=ME)
        h_sb = y_all[:, 15, 0:2 * FF].rearrange("p (r f) -> p r f", r=2)
        sgu = y_all[:, 15, 2 * FF:4 * FF].rearrange("p (r f) -> p r f", r=2)
        ln_r = xs[:, 0:4, :].rearrange("p (r a) d -> p r (a d)", r=2)
        ln_s = sb("ln_s", [P, 2, 6])
        ln_m = sb("ln_m", [P, 2, 2])
        ln_v = sb("ln_v", [P, 2, 2])
        ids_sb = z_gate[:, 0, :].bitcast(I32)
        ge_b = z_gate[:, 1, :].bitcast(BF16)[:, 0:NT]
        w_hi_f, w_lo_f = (t[:, :, :].rearrange("p a w -> p (a w)") for t in (w_hi, w_lo))
        e_hi, e_lo = (t[:, 0:2 * RW].rearrange("p (r w) -> p r w", r=2) for t in (w_hi_f, w_lo_f))
        hT1_hi = sb("hT1_hi", [FH, 512], F32R)
        hT1_lo = sb("hT1_lo", [FH, 512], F32R)
        hT_hi = [w_hi_f[0:FH, 2 * RW:2 * RW + 512], hT1_hi[:, :]]
        hT_lo = [w_lo_f[0:FH, 2 * RW:2 * RW + 512], hT1_lo[:, :]]

        names = ("ld_x ld_c z_const st_cum d_x d_dt a_dt s_dt s_dtT d_dtT "
                 "p_split u_done p_arg s_done xt_done y_done ms_done "
                 "a_copy a_z a_silu a_decay a_sq a_ln a_rs "
                 "v_tap v_xs v_m v_yz v_y "
                 "ld_wo ld_late ln_st "
                 "p_mask v_xm h_done a_sg v_g v_gm "
                 "o0 o1 o2 r0 r1 r2 s0 s1 s2 l0 l1 l2 q0 q1 q2 n0 n1 n2 t0 t1 a_t0 a_t1 v_t1 "
                 "lg_done v_rt a_el v_comb p_ex gu_done a_sgu v_h ht_done a_hT v_hT dn_done st_out")
        S = {n: sem(n) for n in names.split()}
        ld_w = [sem("ld_w0"), sem("ld_w1")]
        ld_cum = [sem("ld_cum0"), sem("ld_cum1")]
        ld_ex = [sem("ld_ex0"), sem("ld_ex1")]
        block = ctx.enter_context(nc.Block())

        def ge(e, s, value):
            if not (isinstance(value, int) and value <= 0):
                e.wait_ge(s, value)

        def steps(e, step, after_first=None):
            step(0, 0, True, False, False)
            if after_first:
                after_first()
            step(1, 1, True, True, False)
            with e.Fori(0, (NPAIR - 2) // 2) as k:
                step(k * 2 + 2, 0, True, True, True)
                step(k * 2 + 3, 1, True, True, True)
            step(NPAIR, 0, False, True, True)
            step(NPAIR + 1, 1, False, False, True)

        def half_read(n, f):
            if f >= 2 * NCONV:
                return S["a_z"], n * 2 + (f - 2 * NCONV) + 1
            return S["v_tap"], n * TAP_N + 4 * (f // 2) + 3 + f % 2

        def experts(e, step):
            step(0, 0, True)
            step(1, 1, False)
            with e.Fori(0, (ME - 3) // 2) as k:
                step(k * 2 + 2, 0, False)
                step(k * 2 + 3, 1, False)
            step(ME - 1, 0, False)

        cols = [(b * T, b * T + P) for b in range(NB)]

        @block.sync
        def _(sp):
            sp.dma_start(xT_raw, xT.rearrange("(k p) t -> p k t", p=P)).then_inc(S["ld_x"], 16)
            sp.dma_start(wdt, wdtT.rearrange("(k p) h -> p k h", p=P)).then_inc(S["ld_c"], 16)
            sp.dma_start(head_c[:, 0:1], dt_bias.rearrange("(h o) -> h o", o=1)).then_inc(S["ld_c"], 16)
            sp.dma_start(head_c[:, 1:2], a_log.rearrange("(h o) -> h o", o=1)).then_inc(S["ld_c"], 16)

            def load_pair(n, par):
                sp.dma_start(w_raw[:, par, :], winT[bass.ds(n, 1)].rearrange("a p w -> p (a w)")
                             ).then_inc(ld_w[par], 16)

            def load_cum(n, par):
                row = cum_dram[bass.ds(2 * n, 2), :].rearrange("(o h) t -> o h t", o=1)
                sp.dma_start(cum_b[:, par, :, :], row.broadcast_to([P, 2, NT])).then_inc(ld_cum[par], 16)

            load_pair(0, 0)
            load_pair(1, 1)
            sp.wait_ge(S["d_dt"], 5)
            sp.dma_start(cum_dram, dt_cum).then_inc(S["st_cum"], 16)
            sp.wait_ge(S["st_cum"], 16)
            load_cum(0, 0)
            load_cum(1, 1)
            with sp.Fori(0, (NPAIR - 2) // 2) as k:
                for par in range(2):
                    n = k * 2 + par
                    ge(sp, S["v_tap"], n * TAP_N + TAP_N)
                    load_pair(n + 2, par)
                    ge(sp, S["p_arg"], n * 3 * NB + 3 * NB)
                    load_cum(n + 2, par)

            sp.wait_ge(S["p_arg"], NPAIR * 3 * NB)
            sp.dma_start(wo_sb, woutT.rearrange("(i p) d -> p i d", p=P)).then_inc(S["ld_wo"], 16)
            sp.wait_ge(S["v_m"], NPAIR * UNITS)
            sp.wait_ge(S["s_done"], NPAIR * UNITS)
            sp.wait_ge(S["v_xs"], 2 * NPAIR)
            sp.wait_ge(S["xt_done"], 2 * NPAIR)
            sp.wait_ge(S["v_y"], 2 * NPAIR)
            sp.dma_start(x_tok, x.rearrange("(b p) d -> p b d", p=P)).then_inc(S["ld_late"], 16)
            sp.dma_start(ids_sb, ids.rearrange("(o t) -> o t", o=1).broadcast_to([P, NT])
                         ).then_inc(S["ld_late"], 16)
            sp.dma_start(ctx_w, ctxT.rearrange("e (k p) f -> p e k f", p=P)).then_inc(S["ld_late"], 16)
            sp.wait_ge(S["o0"], TB)
            sp.dma_start(gate_w, gateT.rearrange("(k p) e -> p k e", p=P)).then_inc(S["ld_late"], 16)
            sp.dma_start(eb_sb, ebias.rearrange("(o e) -> o e", o=1).broadcast_to([P, NE])
                         ).then_inc(S["ld_late"], 16)

            def load_expert(n, par):
                sp.dma_start(exp_raw[:, par, :], wexp[bass.ds(n, 1)].rearrange("a p w -> p (a w)")
                             ).then_inc(ld_ex[par], 16)
            load_expert(0, 0)
            load_expert(1, 1)

            def next_expert(n, par):
                ge(sp, S["p_ex"], n * 2 + 2)
                load_expert(n + 2, par)
            next_expert(0, 0)
            with sp.Fori(0, (ME - 3) // 2) as k:
                next_expert(k * 2 + 1, 1)
                next_expert(k * 2 + 2, 0)
            for b in range(TB):
                sp.wait_ge(S["n2"], b + 1)
                sp.dma_start(out[b * P:(b + 1) * P, :], x1[:, b, :]).then_inc(S["st_out"], 16)
            sp.wait_ge(S["st_out"], 16 * TB)

        @block.gpsimd
        def _(pool):
            made = [0]

            def link(ins):
                made[0] += 1
                ins.then_inc(S["z_const"], 1)
                pool.wait_ge(S["z_const"], made[0])

            link(pool.memset(zero[:, :], 0.0))
            link(pool.memset(ident[:, :], 0.0))
            link(pool.affine_select(out=ident[:, :], in_=ident[:, :], compare_op=ALU.not_equal, fill=1.0,
                                    base=0, pattern=[[-1, P]], channel_multiplier=1))
            link(pool.memset(mean_w[:, :], 0.0))
            link(pool.memset(mean_w[0:HP, 0:HP], 1.0 / HP))
            link(pool.memset(mean_w[HP:P, HP:P], 1.0 / HP))
            link(pool.memset(eps_rms[:, :], RMS_EPS))
            link(pool.memset(eps_ln[:, :], LN_EPS))
            link(pool.memset(mask[:, :], 0.0))
            link(pool.affine_select(out=mask[:, :], in_=mask[:, :], compare_op=ALU.is_ge, fill=NEG,
                                    base=0, pattern=[[1, P]], channel_multiplier=-1))

            def split(n, par):
                pool.wait_ge(ld_w[par], n * 8 + (16 if par == 0 else 8))
                if not (isinstance(n, int) and n < 2):
                    ge(pool, S["u_done"], (n - 1) * 12)
                raw = w_raw[:, par, 0:KD * PW]
                pool.tensor_tensor(w_hi[:, par, :], raw, zero[:, :].broadcast_to([P, KD * PW]), ALU.add).then_inc(S["p_split"], 1)
                ge(pool, S["p_split"], n * 2 + 1)
                pool.tensor_tensor(w_lo[:, par, :], raw, w_hi[:, par, :].bitcast(F32), ALU.subtract
                                   ).then_inc(S["p_split"], 1)

            def log_decay(q, qp, b):
                if b == 0:
                    pool.wait_ge(ld_cum[qp], q * 8 + (16 if qp == 0 else 8))
                if not (isinstance(q, int) and q < 1 and b < 2):
                    ge(pool, S["v_m"], q * UNITS + 2 * b - 2)
                for j, (c, t) in enumerate(((0, T), (T, SC))):
                    pool.tensor_tensor(decay[:, 2 * (b % 2):2 * (b % 2) + 2, c:t],
                                       cum_b[:, qp, :, b * T + j * P:(b + 1) * T],
                                       cum_tok[:, 2 * b + j, bass.ds(q * 2, 2)].unsqueeze(2)
                                       .broadcast_to([P, 2, t - c]), ALU.subtract).then_inc(S["p_arg"], 1)
                ge(pool, S["p_arg"], q * 12 + 3 * b + 2)
                diag = decay[:, 2 * (b % 2):2 * (b % 2) + 2, :].rearrange("p h (j t) -> p h j t", t=P)[:, :, 0:3:2, :]
                pool.tensor_tensor(diag, diag, mask[:, :].unsqueeze(1).unsqueeze(1).broadcast_to([P, 2, 2, P]),
                                   ALU.add).then_inc(S["p_arg"], 1)

            def norm(p, pp, g):
                ge(pool, S["a_rs"], p * 2 + g + 1)
                ge(pool, S["v_yz"], p * 2 + g + 1)
                h = slice(g * 512, (g + 1) * 512)
                dst = y_all[:, bass.ds(p, 1), h].rearrange("p a t -> p (a t)")
                pool.tensor_tensor(dst, z_gate[:, pp, h], y_rs[:, g, :], ALU.mult).then_inc(S["v_y"], 1)

            def step(n, par, split_next, mid, tail):
                if mid:
                    log_decay(n - 1, 1 - par, 0)
                    log_decay(n - 1, 1 - par, 1)
                if split_next:
                    split(n + 1, 1 - par)
                if tail:
                    norm(n - 2, par, 0)
                if mid:
                    log_decay(n - 1, 1 - par, 2)
                    log_decay(n - 1, 1 - par, 3)
                if tail:
                    norm(n - 2, par, 1)

            split(0, 0)
            split(1, 1)
            pool.wait_ge(S["st_cum"], 16)
            pool.wait_ge(S["d_dtT"], 1)
            step(1, 1, True, True, False)
            with pool.Fori(0, (NPAIR - 4) // 2) as k:
                step(k * 2 + 2, 0, True, True, True)
                step(k * 2 + 3, 1, True, True, True)
            step(NPAIR - 2, 0, True, True, True)
            step(NPAIR - 1, 1, False, True, True)
            step(NPAIR, 0, False, True, True)
            step(NPAIR + 1, 1, False, False, True)

            pool.wait_ge(S["ld_late"], 48)
            mk = [0]

            def mlink(ins):
                mk[0] += 1
                ins.then_inc(S["p_mask"], 1)
                pool.wait_ge(S["p_mask"], mk[0])
            mlink(pool.tensor_scalar(emask[:, 0, :], ids_sb, float(TPE), None, ALU.is_lt))
            mlink(pool.tensor_scalar(emask[:, 1, :], ids_sb, float(TPE), None, ALU.is_ge))
            mlink(pool.tensor_scalar(ge_b, ids_sb, float(2 * TPE), None, ALU.is_ge))
            mlink(pool.tensor_scalar(emask[:, 3, :], ids_sb, float(3 * TPE), None, ALU.is_ge))
            mlink(pool.tensor_tensor(emask[:, 1, :], emask[:, 1, :], ge_b, ALU.subtract))
            mlink(pool.tensor_tensor(emask[:, 2, :], ge_b, emask[:, 3, :], ALU.subtract))

            def split_expert(n, par, first=False):
                pool.wait_ge(ld_ex[par], n * 8 + (16 if par == 0 else 8))
                if not (isinstance(n, int) and n < 2):
                    ge(pool, S["dn_done"], (n - 1) * TB)
                raw = exp_raw[:, par, :]
                pool.tensor_tensor(e_hi[:, par, :], raw, zero[:, :].broadcast_to([P, RW]), ALU.add).then_inc(S["p_ex"], 1)
                ge(pool, S["p_ex"], n * 2 + 1)
                pool.tensor_tensor(e_lo[:, par, :], raw, e_hi[:, par, :].bitcast(F32), ALU.subtract
                                   ).then_inc(S["p_ex"], 1)
            pool.wait_ge(S["u_done"], 12 * NPAIR)
            experts(pool, split_expert)

        @block.tensor
        def _(pe):
            pe.wait_ge(S["ld_x"], 16)
            pe.wait_ge(S["ld_c"], 48)
            for hf in range(2):
                for k in range(KD):
                    mm = pe.matmul(ps[0:H, hf, :], wdt[:, k, :], xT_raw[:, k, hf * 512:(hf + 1) * 512],
                                   start=(k == 0), stop=(k == KD - 1))
            mm.then_inc(S["s_dt"], 1)
            def turn_dt():
                pe.wait_ge(S["d_dt"], 5)
                pe.wait_ge(S["z_const"], 8)
                for i, src in enumerate((dt_l, dt_cum)):
                    for b in range(TB):
                        mm = pe.transpose(ps[:, 4 + i, b * H:(b + 1) * H], src[:, b * P:(b + 1) * P],
                                          ident[0:H, 0:H])
                mm.then_inc(S["s_dtT"], 1)
                pe.wait_ge(S["d_dtT"], 1)

            def step(n, par, front, mid, tail):
                q, qp, r = n - 1, 1 - par, n - 2

                def x_to_tokens(c):
                    ge(pe, S["a_silu"], q * NCONV + 1)
                    ge(pe, S["v_m"], q * UNITS - 1 + c)
                    for b in range(4):
                        mm = pe.transpose(ps[:, 4 + c, b * P:(b + 1) * P],
                                          conv[:, qp, 0, (4 * c + b) * P:(4 * c + b + 1) * P], ident[:, :])
                    mm.then_inc(S["xt_done"], 1)

                def project(j):
                    if j >= 4:
                        ge(pe, *half_read(n, j - 4))
                    elif not (isinstance(n, int) and n == 0):
                        ge(pe, *half_read(n - 1, j + 8))
                    tile, hf = j // 2, j % 2
                    i = 0
                    for kk in range(KD):
                        w = slice(kk * PW + tile * P, kk * PW + tile * P + P)
                        t = slice(hf * 512, hf * 512 + 512)
                        for wp, xp in ((w_hi, x_hi), (w_hi, x_lo), (w_lo, x_hi)):
                            mm = pe.matmul(ps[:, j % 4, :], wp[:, par, w], xp[:, kk, t],
                                           start=(i == 0), stop=(i == 5))
                            i += 1
                    mm.then_inc(S["u_done"], 1)

                def score(k):
                    b, h = k // 2, k % 2
                    c0, c1 = cols[b]
                    Bm, Cm = conv[:, qp, 1 + 2 * h, :], conv[:, qp, 2 + 2 * h, :]
                    ge(pe, S["a_silu"], q * NCONV + 3 + 2 * h)
                    if k < 2:
                        ge(pe, S["v_xs"], q * 2 + k + 1)
                    else:
                        ge(pe, S["v_m"], q * UNITS + k - 1)
                    pe.matmul(ps[:, 4 + k % 2, 0:T], Bm[:, c0:c0 + P], Cm[:, c0:c0 + T], start=True, stop=True)
                    pe.matmul(ps[:, 4 + k % 2, T:SC], Bm[:, c1:c1 + P], Cm[:, c1:c1 + P], start=True, stop=True
                              ).then_inc(S["s_done"], 1)

                def mix(p, u):
                    b, h, g = u // 2, u % 2, u // 4
                    y = ps[h * HP:(h + 1) * HP, 6 + g, (b % 2) * T:(b % 2) * T + T]
                    ch = slice(h * HP, (h + 1) * HP)
                    ge(pe, S["v_m"], p * UNITS + u + 1)
                    if u % 4 == 0:
                        ge(pe, S["v_xs"], p * 2 + 1 + g)
                        ge(pe, S["a_ln"], p * 2 - 1 + g)
                    pe.matmul(y, xs[:, 2 * b, ch], scores[:, u % 2, 0:T], start=True, stop=False,
                              skip_group_check=True)
                    pe.matmul(y[:, P:T], xs[:, 2 * b + 1, ch], scores[:, u % 2, T:SC], start=False, stop=True,
                              skip_group_check=True).then_inc(S["y_done"], 1)

                def mean_square(p, g):
                    ge(pe, S["a_sq"], p * 2 + g + 1)
                    ge(pe, S["v_yz"], p * 2 + g + 1)
                    pe.matmul(ps[:, 6 + g, :], mean_w[:, :], y_sq[:, :], start=True, stop=True
                              ).then_inc(S["ms_done"], 1)

                if front:
                    ge(pe, S["p_split"], n * 2 + 2)
                    if isinstance(n, int) and n == 0:
                        ge(pe, S["d_x"], 3)
                for j in range(2 * NTILE):
                    if mid and j < 2:
                        x_to_tokens(j)
                    if front:
                        project(j)
                    if mid and 3 <= j < 3 + UNITS:
                        score(j - 3)
                    if mid and j >= 4:
                        mix(q, j - 4)
                    if tail and j == 3:
                        mean_square(r, 1)
                    if mid and j == 11:
                        mean_square(q, 0)

            steps(pe, step, turn_dt)

            def turn(b, n_sem, a_sem, t_sem, src, bank):
                pe.wait_ge(n_sem, b + 1)
                if b >= 2:
                    pe.wait_ge(a_sem, b - 1)
                for k in range(KD):
                    mm = pe.transpose(ps[:, bank + b % 2, k * P:(k + 1) * P], src[:, b, k * P:(k + 1) * P],
                                      ident[:, :])
                mm.then_inc(t_sem, 1)

            pe.wait_ge(S["v_y"], 2 * NPAIR)
            pe.wait_ge(S["ld_wo"], 16)
            for b in range(TB):
                if b >= 2:
                    ge(pe, S["r0"], b - 1)
                for i in range(NPAIR):
                    mm = pe.matmul(ps[:, b % 2, 0:D], y_all[:, i, b * P:(b + 1) * P], wo_sb[:, i, :],
                                   start=(i == 0), stop=(i == NPAIR - 1))
                mm.then_inc(S["o0"], 1)
                if b >= 1:
                    turn(b - 1, S["n0"], S["a_t0"], S["t0"], x1, 2)
            turn(TB - 1, S["n0"], S["a_t0"], S["t0"], x1, 2)

            pe.wait_ge(S["ld_late"], 48)
            for hf in range(2):
                if hf:
                    pe.wait_ge(S["v_g"], 1)
                for e in range(EX):
                    pe.wait_ge(S["v_xm"], hf * EX + e + 1)
                    for m in range(2):
                        for k in range(KD):
                            mm = pe.matmul(ps[:, 4 + m, :], ctx_w[:, e, k, m * P:(m + 1) * P], xm[:, e % 2, k, :],
                                           start=(e == 0 and k == 0), stop=(e == EX - 1 and k == KD - 1))
                    mm.then_inc(S["h_done"], 1)
                for b in range(4 * hf, 4 * hf + 4):
                    if b >= 2:
                        ge(pe, S["r1"], b - 1)
                    pe.wait_ge(S["v_gm"], hf * EX + EX)
                    for e in range(EX):
                        for k in range(KD):
                            mm = pe.matmul(ps[:, b % 2, 0:D], gm[:, e, k, (b % 4) * P:(b % 4) * P + P],
                                           ctx_w[:, e, k, :], start=(e == 0 and k == 0),
                                           stop=(e == EX - 1 and k == KD - 1))
                    mm.then_inc(S["o1"], 1)
                    if b >= 1:
                        turn(b - 1, S["n1"], S["a_t1"], S["t1"], x2, 2)
            turn(TB - 1, S["n1"], S["a_t1"], S["t1"], x2, 2)

            pe.wait_ge(S["a_t1"], TB)
            pe.wait_ge(S["ld_late"], 80)
            pe.wait_ge(S["r1"], TB)
            for b in range(TB):
                for k in range(KD):
                    mm = pe.matmul(ps[:, 0, b * NE:(b + 1) * NE], x2T[:, k, b * P:(b + 1) * P], gate_w[:, k, :],
                                   start=(k == 0), stop=(k == KD - 1))
            mm.then_inc(S["lg_done"], 1)
            pe.wait_ge(S["v_rt"], 2)
            pe.wait_ge(S["v_t1"], 2)

            def down(n, par, first, b):
                ge(pe, S["v_hT"], n * 4 + b // 2 + 1)
                for k in range(2):
                    hs = slice(((b % 2) * 2 + k) * P, ((b % 2) * 2 + k + 1) * P)
                    ws = slice(KD * 2 * FF + k * D, KD * 2 * FF + (k + 1) * D)
                    for i, (hp, wp) in enumerate(((hT_hi, e_hi), (hT_hi, e_lo), (hT_lo, e_hi))):
                        mm = pe.matmul(ps[:, 4 + b // 2, (b % 2) * D:(b % 2) * D + D], hp[(b // 2) % 2][:, hs],
                                       wp[0:FH, par, ws], start=(first and b % 2 == 0 and k == 0 and i == 0),
                                       stop=False, skip_group_check=True)
                mm.then_inc(S["dn_done"], 1)

            def turn_h(n, b):
                ge(pe, S["v_h"], n * TB + b + 1)
                if b % 2 == 0:
                    ge(pe, S["v_hT"], n * 4 + b // 2 - 1)
                for k in range(2):
                    c = ((b % 2) * 2 + k) * P
                    mm = pe.transpose(ps[0:FH, 2 + (b // 2) % 2, c:c + P], h_sb[:, b % 2, k * FH:(k + 1) * FH],
                                      ident[:, :])
                mm.then_inc(S["ht_done"], 1)

            def expert(n, par, first):
                ge(pe, S["p_ex"], n * 2 + 2)
                for b in range(TB):
                    if not (first and b < 2):
                        ge(pe, S["v_h"], n * TB + b - 1)
                    i = 0
                    for k in range(KD):
                        w = slice(k * 2 * FF, (k + 1) * 2 * FF)
                        for xp, wp in ((x_hi, e_hi), (x_hi, e_lo), (x_lo, e_hi)):
                            mm = pe.matmul(ps[:, b % 2, 0:2 * FF], xp[:, k, b * P:(b + 1) * P], wp[:, par, w],
                                           start=(i == 0), stop=(i == 5))
                            i += 1
                    mm.then_inc(S["gu_done"], 1)
                    if b >= 1:
                        turn_h(n, b - 1)
                    elif not first:
                        turn_h(n - 1, TB - 1)
                    if b >= 4:
                        down(n, par, first, b - 4)
                    elif not first:
                        down(n - 1, 1 - par, isinstance(n, int) and n == 1, b + 4)

            experts(pe, expert)
            turn_h(ME - 1, TB - 1)
            for b in range(4, TB):
                down(ME - 1, 0, False, b)

        @block.scalar
        def _(act):
            act.wait_ge(S["z_const"], 8)
            act.preload_act_table_set("natural_log_exp_and_others")
            act.wait_ge(S["ld_c"], 48)
            act.activation(head_c[:, 2:3], head_c[:, 1:2], ACT.Exp).then_inc(S["a_dt"], 1)
            act.wait_ge(S["a_dt"], 1)
            act.wait_ge(S["d_x"], 4)
            act.activation(dt_e, dt_e, ACT.Exp, scale=-1.0).then_inc(S["a_dt"], 1)
            act.wait_ge(S["a_dt"], 2)
            act.activation(dt_ch, dt_e, ACT.Ln, bias=1.0).then_inc(S["a_dt"], 1)

            def step(n, par, front, mid, tail):
                q, qp, r = n - 1, 1 - par, n - 2

                def silu(p, pp, tile):
                    ge(act, S["v_tap"], p * TAP_N + 4 * (tile + 1))
                    act.activation(conv[:, pp, tile, :], conv[:, pp, tile, :], ACT.Silu).then_inc(S["a_silu"], 1)

                def z(hf):
                    ge(act, S["u_done"], q * 12 + 2 * NCONV + hf + 1)
                    if not (isinstance(q, int) and q < 2):
                        ge(act, S["v_y"], q * 2 - 2)
                    act.activation(z_gate[:, qp, hf * 512:(hf + 1) * 512], ps[:, (2 * NCONV + hf) % 4, :], ACT.Silu
                                   ).then_inc(S["a_z"], 1)

                def copy(j):
                    tile, hf = j // 2, j % 2
                    ge(act, S["u_done"], n * 12 + j + 1)
                    if j == 0 and not (isinstance(n, int) and n < 2):
                        ge(act, S["s_done"], n * UNITS - UNITS)
                    tap = KD * PW + tile * TAPS + TAPS - 1
                    act.activation(conv[:, par, tile, hf * 512:(hf + 1) * 512], ps[:, j % 4, :], ACT.Copy,
                                   scale=w_raw[:, par, tap:tap + 1]).then_inc(S["a_copy"], 1)

                def exp_decay(b):
                    ge(act, S["p_arg"], q * 3 * NB + 3 * b + 3)
                    d = decay[:, 2 * (b % 2):2 * (b % 2) + 2, :]
                    act.activation(d, d, ACT.Exp).then_inc(S["a_decay"], 1)

                def square(p, g):
                    ge(act, S["y_done"], p * UNITS + 4 * g + 4)
                    ge(act, S["ms_done"], p * 2 + g)
                    act.activation(y_sq[:, :], ps[:, 6 + g, :], ACT.Square).then_inc(S["a_sq"], 1)

                def rsqrt(p, g):
                    ge(act, S["ms_done"], p * 2 + g + 1)
                    ge(act, S["v_y"], p * 2)
                    act.activation(y_rs[:, g, :], ps[:, 6 + g, :], ACT.Ln, bias=eps_rms[:, 0:1]).then_inc(S["a_ln"], 1)
                    ge(act, S["a_ln"], p * 2 + g + 1)
                    act.activation(y_rs[:, g, :], y_rs[:, g, :], ACT.Exp, scale=-0.5).then_inc(S["a_rs"], 1)

                if isinstance(n, int) and n == 0:
                    act.preload_act_table_set("silu_and_others")
                if mid:
                    z(0)
                    z(1)
                work = [[] for _ in range(2 * NTILE)]
                if mid:
                    work[0] += [lambda: silu(q, qp, 4)]
                if tail:
                    work[1] += [lambda: square(r, 1)]
                if mid or tail:
                    work[1] += [lambda: act.preload_act_table_set("natural_log_exp_and_others")]
                if mid:
                    for b, j in enumerate((2, 4, 6, 8)):
                        work[j] += [lambda b=b: exp_decay(b)]
                    work[8].insert(0, lambda: square(q, 0))
                if tail:
                    work[3] += [lambda: rsqrt(r, 0)]
                    work[5] += [lambda: rsqrt(r, 1)]
                for j in range(2 * NTILE):
                    if front and j < 2 * NCONV:
                        copy(j)
                    for f in work[j]:
                        f()
                if front:
                    if mid:
                        act.preload_act_table_set("silu_and_others")
                    for tile in range(4):
                        silu(n, par, tile)

            steps(act, step)

            def layer_norm_scale(b, i):
                act.wait_ge(S[f"s{i}"], b + 1)
                act.activation(ln_v[:, b % 2, 0:1], ln_m[:, b % 2, 1:2], ACT.Ln, bias=eps_ln[:, 0:1]
                               ).then_inc(S[f"l{i}"], 1)
                act.wait_ge(S[f"l{i}"], b + 1)
                act.activation(ln_v[:, b % 2, 1:2], ln_v[:, b % 2, 0:1], ACT.Exp, scale=-0.5
                               ).then_inc(S[f"q{i}"], 1)

            def take_turned(b, t_sem, a_sem, dst):
                act.wait_ge(t_sem, b + 1)
                act.activation(dst[:, :, b * P:(b + 1) * P],
                               ps[:, 2 + b % 2, 0:D].rearrange("p (k t) -> p k t", k=KD), ACT.Copy
                               ).then_inc(a_sem, 1)

            for b in range(TB):
                layer_norm_scale(b, 0)
                if b >= 1:
                    take_turned(b - 1, S["t0"], S["a_t0"], x1T)
            take_turned(TB - 1, S["t0"], S["a_t0"], x1T)

            for hf in range(2):
                act.preload_act_table_set("silu_and_others")
                act.wait_ge(S["h_done"], hf * EX + EX)
                act.activation(sg_sb[:, :, :], ps[:, 4:6, :], ACT.Silu).then_inc(S["a_sg"], 1)
                act.preload_act_table_set("natural_log_exp_and_others")
                for b in range(4 * hf, 4 * hf + 4):
                    layer_norm_scale(b, 1)
                    if b >= 1:
                        take_turned(b - 1, S["t1"], S["a_t1"], x2T)
            take_turned(TB - 1, S["t1"], S["a_t1"], x2T)

            act.wait_ge(S["v_rt"], 4)
            act.activation(ew, ew, ACT.Exp).then_inc(S["a_el"], 1)

            act.preload_act_table_set("silu_and_others")

            def expert(n, par, first):
                def take_h(m, c):
                    act.wait_ge(S["ht_done"], m * TB + 2 * c + 2)
                    if not (isinstance(m, int) and m == 0 and c < 2):
                        act.wait_ge(S["dn_done"], m * TB + 2 * c - 2)
                    act.activation(hT_hi[c % 2], ps[0:FH, 2 + c % 2, :], ACT.Copy).then_inc(S["a_hT"], 1)
                for b in range(TB):
                    ge(act, S["gu_done"], n * TB + b + 1)
                    if not (first and b < 2):
                        ge(act, S["v_h"], n * TB + b - 1)
                    act.activation(sgu[:, b % 2, :], ps[:, b % 2, 0:FF], ACT.Silu).then_inc(S["a_sgu"], 1)
                    if b in (2, 4, 6):
                        take_h(n, b // 2 - 1)
                    if b == 0 and not first:
                        take_h(n - 1, 3)
            experts(act, expert)
            act.wait_ge(S["ht_done"], ME * TB)
            act.wait_ge(S["dn_done"], ME * TB - 4)
            act.activation(hT_hi[1], ps[0:FH, 3, :], ACT.Copy).then_inc(S["a_hT"], 1)

            act.preload_act_table_set("natural_log_exp_and_others")
            for b in range(TB):
                layer_norm_scale(b, 2)

        @block.vector
        def _(dve):
            dve.wait_ge(S["ld_x"], 16)
            dve.tensor_copy(x_hi[:, :, :], xT_raw).then_inc(S["d_x"], 1)
            dve.wait_ge(S["d_x"], 1)
            dve.tensor_tensor(x_lo[:, :, :], xT_raw, x_hi[:, :, :].bitcast(F32), ALU.subtract).then_inc(S["d_x"], 1)
            dve.wait_ge(S["ld_c"], 48)
            dve.wait_ge(S["s_dt"], 1)
            dve.tensor_scalar(dt_z, ps[0:H, 0:2, :].rearrange("p a t -> p (a t)"), head_c[:, 0:1], None, ALU.add
                              ).then_inc(S["d_x"], 1)
            dve.wait_ge(S["d_x"], 3)
            dve.scalar_tensor_tensor(out=dt_e, in0=dt_z, scalar=-1.0, in1=dt_z, op0=ALU.mult, op1=ALU.max).then_inc(S["d_x"], 1)
            made = [0]

            def link(ins):
                made[0] += 1
                ins.then_inc(S["d_dt"], 1)
                dve.wait_ge(S["d_dt"], made[0])
            link(dve.tensor_scalar(dt_l, dt_z, 0.0, None, ALU.max))
            dve.wait_ge(S["a_dt"], 3)
            link(dve.tensor_tensor(dt_l, dt_l, dt_ch, ALU.add))
            link(dve.tensor_scalar(dt_da, dt_l, head_c[:, 2:3], -1.0, ALU.mult, ALU.mult))
            link(dve.memset(dt_z, 1.0))
            for b in range(NB):
                t = slice(b * T, (b + 1) * T)
                ins = dve.tensor_tensor_scan(dt_cum[:, t], dt_z[:, t], dt_da[:, t], 0.0, ALU.mult, ALU.add)
            link(ins)

            def take_dt():
                dve.wait_ge(S["s_dtT"], 1)
                dve.tensor_copy(dt_tok[:, :, :], ps[:, 4, 0:TB * H].rearrange("p (b h) -> p b h", b=TB))
                dve.tensor_copy(cum_tok[:, :, :], ps[:, 5, 0:TB * H].rearrange("p (b h) -> p b h", b=TB)
                                ).then_inc(S["d_dtT"], 1)
                dve.wait_ge(S["d_dtT"], 1)

            def step(n, par, front, mid, tail):
                q, qp, r, rp = n - 1, 1 - par, n - 2, par

                def x_scaled(c):
                    ge(dve, S["xt_done"], q * 2 + c + 1)
                    ge(dve, S["y_done"], q * UNITS)
                    dve.tensor_tensor(xs[:, 4 * c:4 * c + 4, :].rearrange("p b (h c) -> p b h c", h=2),
                                      ps[:, 4 + c, :].rearrange("p (b h c) -> p b h c", b=4, h=2),
                                      dt_tok[:, 4 * c:4 * c + 4, bass.ds(q * 2, 2)].unsqueeze(3)
                                      .broadcast_to([P, 4, 2, HP]), ALU.mult).then_inc(S["v_xs"], 1)

                def weigh(k):
                    ge(dve, S["a_decay"], q * NB + k // 2 + 1)
                    ge(dve, S["s_done"], q * UNITS + k + 1)
                    ge(dve, S["y_done"], q * UNITS + max(k - 1, 0))
                    dve.tensor_tensor(scores[:, k % 2, :], ps[:, 4 + k % 2, 0:SC], decay[:, k % 4, :], ALU.mult
                                      ).then_inc(S["v_m"], 1)

                def tap(m, i):
                    s = min(i + 1, 3)
                    halves = slice(0, 2) if i < 2 else slice(i - 2, i - 1)
                    if i == 0:
                        ge(dve, S["a_copy"], n * (2 * NCONV) + 2 * m + 2)
                    else:
                        ge(dve, S["v_tap"], n * TAP_N + 4 * m + min(i, 2))
                    o = conv[:, par, m, :].rearrange("p (b t) -> p b t", b=NB)[:, 2 * halves.start:2 * halves.stop, :]
                    u = ps[:, (2 * m) % 4:(2 * m) % 4 + 2, :].rearrange("p a (b t) -> p (a b) t", b=2)
                    u = u[:, 2 * halves.start:2 * halves.stop, :]
                    c = KD * PW + m * TAPS + TAPS - 1 - s
                    dve.scalar_tensor_tensor(out=o[:, :, s:], in0=u[:, :, 0:T - s],
                                             scalar=w_raw[:, par, c:c + 1], in1=o[:, :, s:],
                                             op0=ALU.mult, op1=ALU.add).then_inc(S["v_tap"], 1)

                def gate(p, pp, g):
                    ge(dve, S["a_z"], p * 2 + g + 1)
                    ge(dve, S["a_sq"], p * 2 + g + 1)
                    dve.tensor_tensor(z_gate[:, pp, g * 512:(g + 1) * 512], ps[:, 6 + g, :], z_gate[:, pp, g * 512:(g + 1) * 512],
                                      ALU.mult).then_inc(S["v_yz"], 1)

                between = {}
                if mid:
                    between[0, 0] = [lambda: x_scaled(0)]
                    between[0, 2] = [lambda: x_scaled(1)]
                    for k, at_ in enumerate(((1, 0), (2, 0), (2, 1), (3, 0), (3, 1), (4, 0), (4, 1), (4, 3))):
                        between[at_] = [lambda k=k: weigh(k)]
                    between[4, 2] = [lambda: gate(q, qp, 0)]
                if tail:
                    between[0, 1] = [lambda: gate(r, rp, 1)]
                for m in range(NCONV):
                    for i in range(4):
                        for f in between.get((m, i), []):
                            f()
                        if front:
                            tap(m, i)
            steps(dve, step, take_dt)

            def layer_norm(b, i, src, res, dst):
                r = ln_r[:, b % 2, :]
                if i < 2:
                    dve.wait_ge(S[f"o{i}"], b + 1)
                dve.tensor_tensor(r, src, res, ALU.add).then_inc(S[f"r{i}"], 1)
                dve.wait_ge(S[f"r{i}"], b + 1)
                stat(dve.bn_stats(ln_s[:, b % 2, :], r))
                dve.bn_aggr(ln_m[:, b % 2, :], ln_s[:, b % 2, :]).then_inc(S[f"s{i}"], 1)
                dve.wait_ge(S[f"q{i}"], b + 1)
                dve.wait_ge(S[f"s{i}"], b + 1)
                dve.tensor_scalar(dst, r, ln_m[:, b % 2, 0:1], ln_v[:, b % 2, 1:2], ALU.subtract, ALU.mult
                                  ).then_inc(S[f"n{i}"], 1)
            stats = [0]

            def stat(ins):
                stats[0] += 1
                ins.then_inc(S["ln_st"], 1)
                dve.wait_ge(S["ln_st"], stats[0])

            dve.wait_ge(S["ld_late"], 48)
            for b in range(TB):
                layer_norm(b, 0, ps[:, b % 2, 0:D], x_tok[:, b, :], x1[:, b, :])

            dve.wait_ge(S["p_mask"], 6)
            dve.wait_ge(S["a_t0"], TB)
            for hf in range(2):
                t = slice(hf * 512, (hf + 1) * 512)
                for e in range(EX):
                    if hf * EX + e >= 2:
                        ge(dve, S["h_done"], hf * EX + e - 1)
                    dve.tensor_tensor(xm[:, e % 2, :, :], x1T[:, :, t],
                                      emask[:, e, t].unsqueeze(1).broadcast_to([P, KD, 512]), ALU.mult
                                      ).then_inc(S["v_xm"], 1)
                dve.wait_ge(S["a_sg"], hf + 1)
                dve.tensor_tensor(g_sb, sg_sb, ps[:, 4:6, :], ALU.mult).then_inc(S["v_g"], 1)
                dve.wait_ge(S["v_g"], hf + 1)
                if hf:
                    dve.wait_ge(S["o1"], 4)
                for e in range(EX):
                    dve.tensor_tensor(gm[:, e, :, :], g_sb,
                                      emask[:, e, t].unsqueeze(1).broadcast_to([P, KD, 512]), ALU.mult
                                      ).then_inc(S["v_gm"], 1)
                for b in range(4 * hf, 4 * hf + 4):
                    layer_norm(b, 1, ps[:, b % 2, 0:D], x1[:, b, :], x2[:, b, :])

            dve.wait_ge(S["a_t1"], TB)
            dve.tensor_copy(x_hi[:, :, :], x2T).then_inc(S["v_t1"], 1)
            dve.wait_ge(S["v_t1"], 1)
            dve.tensor_tensor(x_lo[:, :, :], x2T, x_hi[:, :, :].bitcast(F32), ALU.subtract).then_inc(S["v_t1"], 1)

            made[0] = 0

            def rlink(ins):
                made[0] += 1
                ins.then_inc(S["v_rt"], 1)
                dve.wait_ge(S["v_rt"], made[0])
            dve.wait_ge(S["lg_done"], 1)
            dve.wait_ge(S["ld_late"], 80)
            lg = ps[:, 0, 0:TB * NE].rearrange("p (b e) -> p b e", b=TB)
            rlink(dve.tensor_copy(logit, lg))
            rlink(dve.tensor_tensor(biased[:, :, 0:NE], lg, eb_sb.unsqueeze(1).broadcast_to([P, TB, NE]), ALU.add))
            rlink(dve.tensor_reduce(lmax, logit, AX.X, ALU.max))
            rlink(dve.tensor_tensor(ew, logit, lmax.unsqueeze(2).broadcast_to([P, TB, NE]), ALU.subtract))
            rlink(dve.memset(biased[:, :, NE:NBI], PAD))
            for b in range(TB):
                ins = dve.max(top8[:, b, :], biased[:, b, 0:NE])
            rlink(ins)
            rlink(dve.memset(top8[:, :, 2:8], PAD))
            for b in range(TB):
                ins = dve.match_replace(out=taken[:, b, :], in_to_replace=top8[:, b, :], in_values=biased[:, b, :],
                                        imm_value=HIT)
            rlink(ins)
            rlink(dve.tensor_tensor(taken[:, :, 0:NE], taken[:, :, 0:NE], biased[:, :, 0:NE], ALU.not_equal))
            dve.wait_ge(S["a_el"], 1)
            rlink(dve.tensor_tensor(ew, ew, taken[:, :, 0:NE], ALU.mult))
            rlink(dve.tensor_reduce(lsum, ew, AX.X, ALU.add))
            rlink(dve.reciprocal(lrec, lsum))
            rlink(dve.memset(comb[:, NE, :], 1.0))
            rlink(dve.tensor_tensor(comb[:, 0:NE, :].rearrange("p e b -> p b e"), ew,
                                    lrec.unsqueeze(2).broadcast_to([P, TB, NE]), ALU.mult))

            def expert(n, par, first):
                def take_h(m, c):
                    dve.wait_ge(S["a_hT"], m * 4 + c + 1)
                    dve.tensor_tensor(hT_lo[c % 2], ps[0:FH, 2 + c % 2, :], hT_hi[c % 2].bitcast(F32),
                                      ALU.subtract).then_inc(S["v_hT"], 1)
                for b in range(TB):
                    ge(dve, S["a_sgu"], n * TB + b + 1)
                    if not (first and b < 2):
                        ge(dve, S["ht_done"], n * TB + b - 1)
                    dve.scalar_tensor_tensor(out=h_sb[:, b % 2, :], in0=sgu[:, b % 2, :],
                                             scalar=comb[:, bass.ds(n, 1), b:b + 1].rearrange("p a b -> p (a b)"),
                                             in1=ps[:, b % 2, FF:2 * FF], op0=ALU.mult, op1=ALU.mult
                                             ).then_inc(S["v_h"], 1)
                    if b in (2, 4, 6):
                        take_h(n, b // 2 - 1)
                    if b == 0 and not first:
                        take_h(n - 1, 3)
            experts(dve, expert)
            dve.wait_ge(S["a_hT"], ME * 4)
            dve.tensor_tensor(hT_lo[1], ps[0:FH, 3, :], hT_hi[1].bitcast(F32), ALU.subtract
                              ).then_inc(S["v_hT"], 1)
            dve.wait_ge(S["dn_done"], ME * TB)
            for b in range(TB):
                layer_norm(b, 2, ps[:, 4 + b // 2, (b % 2) * D:(b % 2) * D + D], x2[:, b, :], x1[:, b, :])


_OUT = (NB, T, D)


def kernel(**inputs):
    import numpy as np
    import concourse.bacc as bacc
    from concourse.bass_utils import run_bass_kernel_spmd

    g = {k: np.asarray(v) for k, v in inputs.items()}
    x = g["x"].reshape(NT, D)
    win = g["L0_attn_Win"]
    o_z, o_b, o_c, o_dt = H * HP, 2 * H * HP, 2 * H * HP + H * N, 2 * H * HP + 2 * H * N

    def rows(i):
        t = [win[P * i:][:P]]
        for h in (2 * i, 2 * i + 1):
            t += [win[o_b + N * h:][:N], win[o_c + N * h:][:N]]
        t += [win[o_z + P * i:][:P]]
        return np.concatenate(t, 0)
    cx = g["L0_attn_conv_w_x"].reshape(NPAIR, P, TAPS)
    cb, cc = g["L0_attn_conv_w_b"], g["L0_attn_conv_w_c"]
    pairs = []
    for i in range(NPAIR):
        w = rows(i).T.reshape(KD, P, PW).transpose(1, 0, 2).reshape(P, KD * PW)
        taps = [cx[i], cb[2 * i], cc[2 * i], cb[2 * i + 1], cc[2 * i + 1]]
        pairs.append(np.concatenate([w] + taps, 1))
    wg = np.concatenate([g["L0_ffn_w_gate"], g["L0_ffn_sw_gate"][None]], 0)
    wu = np.concatenate([g["L0_ffn_w_up"], g["L0_ffn_sw_up"][None]], 0)
    wd = np.concatenate([g["L0_ffn_w_down"], g["L0_ffn_sw_down"][None]], 0)
    gu = np.concatenate([wg, wu], 1).transpose(0, 2, 1).reshape(ME, KD, P, 2 * FF)
    gu = gu.transpose(0, 2, 1, 3).reshape(ME, P, KD * 2 * FF)
    dn = np.zeros((ME, P, 2 * D), wd.dtype)
    dn[:, :FH] = wd.transpose(0, 2, 1).reshape(ME, 2, FH, D).transpose(0, 2, 1, 3).reshape(ME, FH, 2 * D)
    arrays = {
        "xT": x.T, "x": x, "winT": np.stack(pairs), "wdtT": win[o_dt:].T,
        "a_log": g["L0_attn_A_log"], "dt_bias": g["L0_attn_dt_bias"], "woutT": g["L0_attn_Wout"].T,
        "ids": g["itok_BxS_13_99985"].reshape(NT), "ctxT": g["ctx_2048"].transpose(0, 2, 1),
        "gateT": g["L0_ffn_gate_w"].T, "ebias": g["L0_ffn_expert_bias"],
        "wexp": np.concatenate([gu, dn], 2),
    }
    arrays = {f"in_{k}": np.ascontiguousarray(v) for k, v in arrays.items()}
    nc = bacc.Bacc("TRN2", target_bir_lowering=False, num_devices=1)
    args = [nc.dram_tensor(n, a.shape, mybir.dt.from_np(a.dtype), kind="ExternalInput").ap()
            for n, a in arrays.items()]
    out = nc.dram_tensor("out", (NT, D), F32, kind="ExternalOutput").ap()
    build_layer(nc, *args, out)
    r = run_bass_kernel_spmd(nc, [arrays], core_ids=[0])
    return r.results[0]["out"].reshape(_OUT)
```

```python
import concourse.bass as bass
from concourse import mybir
from contextlib import ExitStack

F32 = mybir.dt.float32
F32R = mybir.dt.float32r
BF16 = mybir.dt.bfloat16
I32 = mybir.dt.int32
ALU = mybir.AluOpType
ACT = mybir.ActivationFunctionType
AX = mybir.AxisListType

P = 128
NB, T, D = 4, 256, 256
NT = NB * T
TB = NT // P
KD = D // P
H, HP, N, TAPS = 32, 64, 128, 4
NPAIR = H // 2
NTILE = 6
NCONV = NTILE - 1
PW = NTILE * P
RAWW = KD * PW + NCONV * TAPS
TAPS_OF = [[(slice(h, h + 1), s) for h in (0, 1) for s in (1, 2, 3)] if m == 0 else
           [(slice(0, 2), 1), (slice(0, 2), 2), (slice(0, 1), 3), (slice(1, 2), 3)] for m in range(NCONV)]
TAP_AT = [sum(len(t) for t in TAPS_OF[:m]) for m in range(NCONV + 1)]
TAP_N = TAP_AT[NCONV]
UNITS = 2 * NB
SC = T + P
EX = 4
VOCAB = 12500
TPE = VOCAB // EX
NE, FF = 16, 176
FT = FF - P
UP = 64
GU = ((0, P), (P, 2 * P), (2 * P, 2 * P + UP + FT))
GW = GU[2][1]
ME = NE + 1
RW = KD * GW + 2 * D
NEG = -1.0e30
PAD = -3.0e38
HIT = 3.0e38
LN_EPS = 1e-5
RMS_EPS = 1e-6


def build_layer(nc, xT, x, winT, wdtT, a_log, dt_bias, woutT, ids, ctxT, gateT, ebias, wexp, out):
    comb_dram = nc.dram_tensor("comb_scratch", (NE, NT), F32, kind="Internal").ap()
    cum_dram = nc.dram_tensor("cum_scratch", (H, NT), F32, kind="Internal").ap()

    with ExitStack() as ctx:
        def sb(name, shape, dt=F32):
            return ctx.enter_context(nc.sbuf_tensor(name, shape, dt))

        def sem(name):
            return ctx.enter_context(nc.semaphore(name))

        ps = ctx.enter_context(nc.psum_tensor("ps", [P, 8, 512], F32))

        x_hi = sb("x_hi", [P, KD, NT], F32R)
        x_lo = sb("x_lo", [P, KD, NT], F32R)
        w_raw = sb("w_raw", [P, 2, RAWW])
        conv = sb("conv", [P, 2, NCONV, NT])
        z_gate = sb("z_gate", [P, 2, NT])
        xs = sb("xs", [P, TB, P])
        scores = sb("scores", [P, 2, SC])
        y_all = sb("y_all", [P, NPAIR, NT])
        y_sq = sb("y_sq", [P, 512])
        y_rs = sb("y_rs", [P, 2, 512])
        cum_b = sb("cum_b", [P, 2, 2, NT])
        dt_tok = sb("dt_tok", [P, TB, H])
        cum_tok = sb("cum_tok", [P, TB, H])
        ident = sb("ident", [P, P])
        mean_w = sb("mean_w", [P, P])
        mask = sb("mask", [P, P])
        eps_rms = sb("eps_rms", [P, 1])
        eps_ln = sb("eps_ln", [P, 1])
        zero = sb("zero", [P, 1])
        one = sb("one", [H, 1])
        head_c = sb("head_c", [H, 3])
        ln_s = sb("ln_s", [P, 2, 6])
        ln_m = sb("ln_m", [P, 2, 2])
        ln_v = sb("ln_v", [P, 2, 2])
        h_r = sb("h_r", [P, 2, 512], F32R)
        with ExitStack() as mixer:
            w_hi, w_lo, decay = (mixer.enter_context(nc.sbuf_tensor(name, shape, dt)) for name, shape, dt in
                                 (("w_hi", [P, 2, KD * PW], F32R), ("w_lo", [P, 2, KD * PW], F32R),
                                  ("decay", [P, 4, SC], F32)))
        wo_sb = sb("wo_sb", [P, NPAIR, D])
        sb("spacer", [P, 4 * KD * PW - NPAIR * D])
        h_tail = sb("h_tail", [UP + FT, 2, 512], F32R)

        xT_raw = y_all[:, 0:2, :]
        wdt = y_all[:, 2, 0:KD * H].rearrange("p (k h) -> p k h", k=KD)
        dt_e, dt_l, dt_ch, dt_da, dt_cum = (y_all[0:H, 3 + i, :] for i in range(5))

        conv_f = conv[:, :, :, :].rearrange("p a b t -> p (a b t)")
        at = [0]

        def carve(n):
            at[0] += n
            return conv_f[:, at[0] - n:at[0]]
        x_tok = carve(TB * D).rearrange("p (b d) -> p b d", b=TB)
        x1 = carve(TB * D).rearrange("p (b d) -> p b d", b=TB)
        x2 = x_tok
        x1T = carve(KD * NT).rearrange("p (k t) -> p k t", k=KD)
        ctx_w = carve(EX * KD * D).rearrange("p (e k f) -> p e k f", e=EX, k=KD)
        xm = w_raw[:, :, 0:KD * 512].rearrange("p r (k t) -> p r k t", k=KD)
        emask = carve(EX * NT // 2).bitcast(BF16).rearrange("p (e t) -> p e t", e=EX)
        gm = [t.rearrange("p e (k t) -> p e k t", k=KD) for t in
              (y_all[:, 0:4, :], cum_b[:, :, :, :].rearrange("p a b t -> p (a b) t"))]
        g_sb = y_all[:, 4, :].rearrange("p (k t) -> p k t", k=KD)
        sg_sb = y_all[:, 5, :].rearrange("p (k t) -> p k t", k=KD)
        x2T = y_all[:, 6:8, :]
        exp_raw = y_all[:, 8:12, :].rearrange("p a t -> p (a t)")[:, 0:2 * RW].rearrange("p (r w) -> p r w", r=2)
        gate_w = y_all[:, 12, 0:KD * NE].rearrange("p (k e) -> p k e", k=KD)
        eb_sb = y_all[:, 12, 64:64 + NE]
        r0 = y_all[:, 13, :]
        NBI = NE + 6
        biased = r0[:, 0:TB * NBI].rearrange("p (b e) -> p b e", b=TB)
        taken = r0[:, 256:256 + TB * NBI].rearrange("p (b e) -> p b e", b=TB)
        top8 = r0[:, 512:512 + TB * 8].rearrange("p (b e) -> p b e", b=TB)
        logit = r0[:, 640:640 + TB * NE].rearrange("p (b e) -> p b e", b=TB)
        ew = r0[:, 768:768 + TB * NE].rearrange("p (b e) -> p b e", b=TB)
        lmax = r0[:, 900:900 + TB]
        lsum = r0[:, 908:908 + TB]
        lrec = r0[:, 916:916 + TB]
        comb = y_all[:, 14, 0:NE * TB].rearrange("p (e b) -> p e b", e=NE)
        comb_t = y_all[:, 14, 256:256 + NE * TB]
        h_a = y_all[:, 0, :].rearrange("p (r t) -> p r t", r=2)
        h_b = y_all[:, 1, :].rearrange("p (r t) -> p r t", r=2)
        comb_b = y_all[:, 2:4, :]
        ln_r = xs[:, 0:4, :].rearrange("p (r a) d -> p r (a d)", r=2)
        ids_sb = z_gate[:, 0, :].bitcast(I32)
        ge_b = z_gate[:, 1, :].bitcast(BF16)[:, 0:NT]
        w_hi_f, w_lo_f = (t[:, :, :].rearrange("p a w -> p (a w)") for t in (w_hi, w_lo))
        e_hi, e_lo = (t[:, 0:2 * RW].rearrange("p (r w) -> p r w", r=2) for t in (w_hi_f, w_lo_f))
        a_hi = [h_r[:, 0, :], w_hi_f[:, 2 * RW:2 * RW + 512]]
        a_lo = [h_r[:, 1, :], w_lo_f[:, 2 * RW:2 * RW + 512]]

        names = ("ld_x ld_c z_const st_cum d_x d_dt a_dt s_dt s_dtT d_dtT "
                 "w_split u_done p_arg s_done xt_done y_done ms_done "
                 "a_copy a_z a_silu a_decay a_sq a_ln a_rs "
                 "v_tap v_xs v_m v_yz p_y "
                 "ld_wo ld_xt ld_late ld_rt ln_st "
                 "p_mask v_xm h_done a_sg v_g v_gm "
                 "o0 o1 o2 r0 r1 r2 s0 s1 s2 l0 l1 l2 q0 q1 q2 n0 n1 n2 t0 t1 a_t0 a_t1 v_t1 "
                 "lg_done v_rt a_el v_comb p_ex p_tail gu_done a_s v_t v_w a_hi v_lo s_ct v_ct st_comb dn_done st_out")
        S = {n: sem(n) for n in names.split()}
        ld_w = [sem("ld_w0"), sem("ld_w1")]
        ld_cum = [sem("ld_cum0"), sem("ld_cum1")]
        ld_ex = [sem("ld_ex0"), sem("ld_ex1")]
        ld_cb = [sem("ld_cb0"), sem("ld_cb1")]
        block = ctx.enter_context(nc.Block())

        def ge(e, s, value):
            if not (isinstance(value, int) and value <= 0):
                e.wait_ge(s, value)

        def steps(e, step, after_first=None):
            step(0, 0, True, False, False)
            if after_first:
                after_first()
            step(1, 1, True, True, False)
            with e.Fori(0, (NPAIR - 2) // 2) as k:
                step(k * 2 + 2, 0, True, True, True)
                step(k * 2 + 3, 1, True, True, True)
            step(NPAIR, 0, False, True, True)
            step(NPAIR + 1, 1, False, False, True)

        def half_read(n, f):
            if f >= 2 * NCONV:
                return S["a_z"], n * 2 + (f - 2 * NCONV) + 1
            m, h = f // 2, f % 2
            return S["v_tap"], n * TAP_N + TAP_AT[m] + 1 + [
                i for i, (on, s) in enumerate(TAPS_OF[m]) if s == TAPS - 1 and on.start == h][0]

        def t1_bank(b):
            return 6 if b == TB - 2 else 2 + b % 2

        def hidden_read(j, t):
            return (S["a_s"], j * 2 + 1) if t == 0 else (S["v_t"], j * 2 + t)

        def experts(e, step):
            step(0, 0, True)
            step(1, 1, False)
            with e.Fori(0, (ME - 3) // 2) as k:
                step(k * 2 + 2, 0, False)
                step(k * 2 + 3, 1, False)
            step(ME - 1, 0, False)

        cols = [(b * T, b * T + P) for b in range(NB)]

        def o1_bank(b):
            return (0, 1, 4, 5)[b % 4]

        @block.sync
        def _(sp):
            sp.dma_start(xT_raw, xT.rearrange("(k p) t -> p k t", p=P)).then_inc(S["ld_x"], 16)
            sp.dma_start(wdt, wdtT.rearrange("(k p) h -> p k h", p=P)).then_inc(S["ld_c"], 16)
            sp.dma_start(head_c[:, 0:1], dt_bias.rearrange("(h o) -> h o", o=1)).then_inc(S["ld_c"], 16)
            sp.dma_start(head_c[:, 1:2], a_log.rearrange("(h o) -> h o", o=1)).then_inc(S["ld_c"], 16)

            def load_pair(n, par):
                sp.dma_start(w_raw[:, par, :], winT[bass.ds(n, 1)].rearrange("a p w -> p (a w)")
                             ).then_inc(ld_w[par], 16)

            def load_cum(n, par):
                row = cum_dram[bass.ds(2 * n, 2), :].rearrange("(o h) t -> o h t", o=1)
                sp.dma_start(cum_b[:, par, :, :], row.broadcast_to([P, 2, NT])).then_inc(ld_cum[par], 16)

            load_pair(0, 0)
            load_pair(1, 1)
            sp.wait_ge(S["d_dt"], 3)
            sp.dma_start(cum_dram, dt_cum).then_inc(S["st_cum"], 16)
            sp.wait_ge(S["st_cum"], 16)
            load_cum(0, 0)
            load_cum(1, 1)
            with sp.Fori(0, (NPAIR - 2) // 2) as k:
                for par in range(2):
                    n = k * 2 + par
                    ge(sp, S["v_tap"], n * TAP_N + TAP_N)
                    load_pair(n + 2, par)
                    ge(sp, S["p_arg"], n * 3 * NB + 3 * NB)
                    load_cum(n + 2, par)

            sp.wait_ge(S["u_done"], NPAIR * 2 * NTILE)
            sp.dma_start(wo_sb[:, :, :], woutT.rearrange("(i p) d -> p i d", p=P)).then_inc(S["ld_wo"], 16)
            sp.wait_ge(S["s_done"], NPAIR * UNITS)
            sp.wait_ge(S["xt_done"], 2 * NPAIR)
            sp.dma_start(x_tok, x.rearrange("(b p) d -> p b d", p=P)).then_inc(S["ld_xt"], 16)
            sp.dma_start(ctx_w, ctxT.rearrange("e (k p) f -> p e k f", p=P)).then_inc(S["ld_late"], 16)
            sp.wait_ge(S["p_y"], 2 * NPAIR)
            sp.dma_start(ids_sb, ids.rearrange("(o t) -> o t", o=1).broadcast_to([P, NT])
                         ).then_inc(S["ld_late"], 16)
            sp.wait_ge(S["o0"], TB)
            sp.dma_start(gate_w, gateT.rearrange("(k p) e -> p k e", p=P)).then_inc(S["ld_rt"], 16)
            sp.dma_start(eb_sb, ebias.rearrange("(o e) -> o e", o=1).broadcast_to([P, NE])
                         ).then_inc(S["ld_rt"], 16)

            def load_expert(n, par):
                sp.dma_start(exp_raw[:, par, :], wexp[bass.ds(n, 1)].rearrange("a p w -> p (a w)")
                             ).then_inc(ld_ex[par], 16)
            load_expert(0, 0)
            load_expert(1, 1)

            def next_expert(n, par):
                ge(sp, S["p_ex"], n * 2 + 2)
                load_expert(n + 2, par)

            def load_comb(n, par):
                sp.dma_start(comb_b[:, par, :], comb_dram[bass.ds(n - 1, 1), :].broadcast_to([P, NT])
                             ).then_inc(ld_cb[par], 16)
            next_expert(0, 0)
            sp.wait_ge(S["v_ct"], 1)
            sp.dma_start(comb_dram.rearrange("e (b t) -> (e b) t", b=TB), comb_t).then_inc(S["st_comb"], 16)
            sp.wait_ge(S["st_comb"], 16)
            load_comb(1, 1)
            load_comb(2, 0)
            with sp.Fori(0, (ME - 3) // 2) as k:
                for par in (1, 0):
                    n = k * 2 + 2 - par
                    next_expert(n, par)
                    ge(sp, S["v_w"], n * 4)
                    load_comb(n + 2, par)
            for b in range(TB):
                sp.wait_ge(S["n2"], b + 1)
                sp.dma_start(out[b * P:(b + 1) * P, :], x1[:, b, :]).then_inc(S["st_out"], 16)
            sp.wait_ge(S["st_out"], 16 * TB)

        @block.gpsimd
        def _(pool):
            made = [0]

            def link(ins):
                made[0] += 1
                ins.then_inc(S["z_const"], 1)
                pool.wait_ge(S["z_const"], made[0])

            link(pool.memset(zero[:, :], 0.0))
            link(pool.memset(ident[:, :], 0.0))
            link(pool.memset(one[:, :], 1.0))
            link(pool.affine_select(out=ident[:, :], in_=ident[:, :], compare_op=ALU.not_equal, fill=1.0,
                                    base=0, pattern=[[-1, P]], channel_multiplier=1))
            link(pool.memset(mean_w[:, :], 0.0))
            link(pool.memset(mean_w[0:HP, 0:HP], 1.0 / HP))
            link(pool.memset(mean_w[HP:P, HP:P], 1.0 / HP))
            link(pool.memset(eps_rms[:, :], RMS_EPS))
            link(pool.memset(eps_ln[:, :], LN_EPS))
            link(pool.memset(mask[:, :], 0.0))
            link(pool.affine_select(out=mask[:, :], in_=mask[:, :], compare_op=ALU.is_ge, fill=NEG,
                                    base=0, pattern=[[1, P]], channel_multiplier=-1))

            def split(n, par):
                pool.wait_ge(ld_w[par], n * 8 + (16 if par == 0 else 8))
                if not (isinstance(n, int) and n < 2):
                    ge(pool, S["u_done"], (n - 1) * 12)
                raw = w_raw[:, par, 0:KD * PW]
                pool.tensor_tensor(w_hi[:, par, :], raw, zero[:, :].broadcast_to([P, KD * PW]), ALU.add
                                   ).then_inc(S["w_split"], 1)
                ge(pool, S["w_split"], n * 2 + 1)
                pool.tensor_tensor(w_lo[:, par, :], raw, w_hi[:, par, :].bitcast(F32), ALU.subtract
                                   ).then_inc(S["w_split"], 1)

            def log_decay(q, qp, b):
                if b == 0:
                    pool.wait_ge(ld_cum[qp], q * 8 + (16 if qp == 0 else 8))
                if not (isinstance(q, int) and q < 1 and b < 2):
                    ge(pool, S["v_m"], q * UNITS + 2 * b - 2)
                for j, (c, t) in enumerate(((0, T), (T, SC))):
                    pool.tensor_tensor(decay[:, 2 * (b % 2):2 * (b % 2) + 2, c:t],
                                       cum_b[:, qp, :, b * T + j * P:(b + 1) * T],
                                       cum_tok[:, 2 * b + j, bass.ds(q * 2, 2)].unsqueeze(2)
                                       .broadcast_to([P, 2, t - c]), ALU.subtract).then_inc(S["p_arg"], 1)
                ge(pool, S["p_arg"], q * 12 + 3 * b + 2)
                diag = decay[:, 2 * (b % 2):2 * (b % 2) + 2, :].rearrange("p h (j t) -> p h j t", t=P)[:, :, 0:3:2, :]
                pool.tensor_tensor(diag, diag, mask[:, :].unsqueeze(1).unsqueeze(1).broadcast_to([P, 2, 2, P]),
                                   ALU.add).then_inc(S["p_arg"], 1)

            def norm(p, pp, g):
                ge(pool, S["a_rs"], p * 2 + g + 1)
                ge(pool, S["v_yz"], p * 2 + g + 1)
                h = slice(g * 512, (g + 1) * 512)
                dst = y_all[:, bass.ds(p, 1), h].rearrange("p a t -> p (a t)")
                pool.tensor_tensor(dst, z_gate[:, pp, h], y_rs[:, g, :], ALU.mult).then_inc(S["p_y"], 1)

            def step(n, par, split_next, mid, tail):
                if mid:
                    log_decay(n - 1, 1 - par, 0)
                    log_decay(n - 1, 1 - par, 1)
                if split_next:
                    split(n + 1, 1 - par)
                if tail:
                    norm(n - 2, par, 0)
                if mid:
                    log_decay(n - 1, 1 - par, 2)
                    log_decay(n - 1, 1 - par, 3)
                if tail:
                    norm(n - 2, par, 1)

            pool.wait_ge(S["w_split"], 2)
            split(1, 1)
            pool.wait_ge(S["st_cum"], 16)
            pool.wait_ge(S["d_dtT"], 1)
            step(1, 1, True, True, False)
            with pool.Fori(0, (NPAIR - 4) // 2) as k:
                step(k * 2 + 2, 0, True, True, True)
                step(k * 2 + 3, 1, True, True, True)
            step(NPAIR - 2, 0, True, True, True)
            step(NPAIR - 1, 1, False, True, True)
            step(NPAIR, 0, False, True, True)
            step(NPAIR + 1, 1, False, False, True)

            pool.wait_ge(S["ld_late"], 32)
            mk = [0]

            def mlink(ins):
                mk[0] += 1
                ins.then_inc(S["p_mask"], 1)
                pool.wait_ge(S["p_mask"], mk[0])
            mlink(pool.tensor_scalar(emask[:, 0, :], ids_sb, float(TPE), None, ALU.is_lt))
            mlink(pool.tensor_scalar(emask[:, 1, :], ids_sb, float(TPE), None, ALU.is_ge))
            mlink(pool.tensor_scalar(ge_b, ids_sb, float(2 * TPE), None, ALU.is_ge))
            mlink(pool.tensor_scalar(emask[:, 3, :], ids_sb, float(3 * TPE), None, ALU.is_ge))
            mlink(pool.tensor_tensor(emask[:, 1, :], emask[:, 1, :], ge_b, ALU.subtract))
            mlink(pool.tensor_tensor(emask[:, 2, :], ge_b, emask[:, 3, :], ALU.subtract))

            def split_expert(n, par, first=False):
                pool.wait_ge(ld_ex[par], n * 8 + (16 if par == 0 else 8))
                if not (isinstance(n, int) and n < 2):
                    ge(pool, S["dn_done"], (n - 1) * TB)
                raw = exp_raw[:, par, :]
                pool.tensor_tensor(e_hi[:, par, :], raw, zero[:, :].broadcast_to([P, RW]), ALU.add).then_inc(S["p_ex"], 1)
                ge(pool, S["p_ex"], n * 2 + 1)
                pool.tensor_tensor(e_lo[:, par, :], raw, e_hi[:, par, :].bitcast(F32), ALU.subtract
                                   ).then_inc(S["p_ex"], 1)
            pool.wait_ge(S["u_done"], 12 * NPAIR)
            gap = h_tail[32:UP, :, :].rearrange("p r t -> p (r t)")
            z = zero[32:UP, :].broadcast_to([UP - 32, 1024])
            pool.tensor_tensor(gap, z, z, ALU.add).then_inc(S["p_tail"], 1)
            pool.wait_ge(S["p_tail"], 1)
            experts(pool, split_expert)

        @block.tensor
        def _(pe):
            pe.wait_ge(S["ld_x"], 16)
            pe.wait_ge(S["ld_c"], 48)
            for hf in range(2):
                for k in range(KD):
                    mm = pe.matmul(ps[0:H, 4 + hf, :], wdt[:, k, :], xT_raw[:, k, hf * 512:(hf + 1) * 512],
                                   start=(k == 0), stop=(k == KD - 1))
            mm.then_inc(S["s_dt"], 1)

            def turn_dt():
                pe.wait_ge(S["d_dt"], 3)
                pe.wait_ge(S["z_const"], 9)
                for i, src in enumerate((dt_l, dt_cum)):
                    for b in range(TB):
                        mm = pe.transpose(ps[:, 4 + i, b * H:(b + 1) * H], src[:, b * P:(b + 1) * P],
                                          ident[0:H, 0:H])
                mm.then_inc(S["s_dtT"], 1)
                pe.wait_ge(S["d_dtT"], 1)

            def out_project(b, first, end):
                if first == 0:
                    pe.wait_ge(S["ld_wo"], 16)
                    pe.wait_ge(S["p_y"], 2 * NPAIR - 2)
                if end == NPAIR:
                    pe.wait_ge(S["p_y"], 2 * NPAIR - 1 + b // 4)
                for i in range(first, end):
                    mm = pe.matmul(ps[:, b % 2, 0:D], y_all[:, i, b * P:(b + 1) * P], wo_sb[:, i, :],
                                   start=(i == 0), stop=(i == NPAIR - 1))
                if end == NPAIR:
                    mm.then_inc(S["o0"], 1)

            def step(n, par, front, mid, tail):
                q, qp, r = n - 1, 1 - par, n - 2

                def x_to_tokens(c):
                    ge(pe, S["a_silu"], q * NCONV + 1)
                    ge(pe, S["v_m"], q * UNITS - 1 + c)
                    for b in range(4):
                        mm = pe.transpose(ps[:, 4 + c, b * P:(b + 1) * P],
                                          conv[:, qp, 0, (4 * c + b) * P:(4 * c + b + 1) * P], ident[:, :])
                    mm.then_inc(S["xt_done"], 1)

                def project(j):
                    if j >= 4:
                        ge(pe, *half_read(n, j - 4))
                    elif not (isinstance(n, int) and n == 0):
                        ge(pe, *half_read(n - 1, j + 8))
                    tile, hf = j // 2, j % 2
                    i = 0
                    for kk in range(KD):
                        w = slice(kk * PW + tile * P, kk * PW + tile * P + P)
                        t = slice(hf * 512, hf * 512 + 512)
                        for wp, xp in ((w_hi, x_hi), (w_hi, x_lo), (w_lo, x_hi)):
                            mm = pe.matmul(ps[:, j % 4, :], wp[:, par, w], xp[:, kk, t],
                                           start=(i == 0), stop=(i == 5))
                            i += 1
                    mm.then_inc(S["u_done"], 1)

                def score(k):
                    b, h = k // 2, k % 2
                    c0, c1 = cols[b]
                    Bm, Cm = conv[:, qp, 1 + 2 * h, :], conv[:, qp, 2 + 2 * h, :]
                    ge(pe, S["a_silu"], q * NCONV + 3 + 2 * h)
                    if k < 2:
                        ge(pe, S["v_xs"], q * 2 + k + 1)
                    else:
                        ge(pe, S["v_m"], q * UNITS + k - 1)
                    pe.matmul(ps[:, 4 + k % 2, 0:T], Bm[:, c0:c0 + P], Cm[:, c0:c0 + T], start=True, stop=True)
                    pe.matmul(ps[:, 4 + k % 2, T:SC], Bm[:, c1:c1 + P], Cm[:, c1:c1 + P], start=True, stop=True
                              ).then_inc(S["s_done"], 1)

                def mix(p, u):
                    b, h, g = u // 2, u % 2, u // 4
                    y = ps[h * HP:(h + 1) * HP, 6 + g, (b % 2) * T:(b % 2) * T + T]
                    ch = slice(h * HP, (h + 1) * HP)
                    ge(pe, S["v_m"], p * UNITS + u + 1)
                    if u % 4 == 0:
                        ge(pe, S["v_xs"], p * 2 + 1 + g)
                        ge(pe, S["a_ln"], p * 2 - 1 + g)
                    pe.matmul(y, xs[:, 2 * b, ch], scores[:, u % 2, 0:T], start=True, stop=False,
                              skip_group_check=True)
                    pe.matmul(y[:, P:T], xs[:, 2 * b + 1, ch], scores[:, u % 2, T:SC], start=False, stop=True,
                              skip_group_check=True).then_inc(S["y_done"], 1)

                def mean_square(p, g):
                    ge(pe, S["a_sq"], p * 2 + g + 1)
                    ge(pe, S["v_yz"], p * 2 + g + 1)
                    pe.matmul(ps[:, 6 + g, :], mean_w[:, :], y_sq[:, :], start=True, stop=True
                              ).then_inc(S["ms_done"], 1)

                if front:
                    ge(pe, S["w_split"], n * 2 + 2)
                    if isinstance(n, int) and n == 0:
                        pe.wait_ge(S["d_x"], 2)
                for j in range(2 * NTILE):
                    if front:
                        project(j)
                    if tail and j == 0:
                        mix(r, 7)
                        mean_square(r, 0)
                        if isinstance(n, int) and n == NPAIR + 1:
                            pe.wait_ge(S["a_z"], 2 * NPAIR)
                            out_project(0, 0, NPAIR - 1)
                    if mid and j < 2:
                        x_to_tokens(j)
                    if mid and 3 <= j < 3 + UNITS:
                        score(j - 3)
                    if mid and 4 <= j < 3 + UNITS:
                        mix(q, j - 4)
                    if tail and j == 3:
                        mean_square(r, 1)

            steps(pe, step, turn_dt)

            def turn(b, n_sem, a_sem, t_sem, src, bank):
                pe.wait_ge(n_sem, b + 1)
                if b >= 2:
                    pe.wait_ge(a_sem, b - 1)
                for k in range(KD):
                    mm = pe.transpose(ps[:, bank, k * P:(k + 1) * P], src[:, b, k * P:(k + 1) * P],
                                      ident[:, :])
                mm.then_inc(t_sem, 1)

            out_project(1, 0, NPAIR - 1)
            for b in range(TB):
                if b >= 2:
                    ge(pe, S["r0"], b - 1)
                out_project(b, NPAIR - 1 if b < 2 else 0, NPAIR)
                if b >= 2:
                    turn(b - 2, S["n0"], S["a_t0"], S["t0"], x1, 2 + b % 2)

            pe.wait_ge(S["ld_late"], 32)
            for hf in range(2):
                for e in range(EX):
                    pe.wait_ge(S["v_xm"], hf * EX + e + 1)
                    for m in range(2):
                        for k in range(KD):
                            mm = pe.matmul(ps[:, 4 + 2 * hf + m, :], ctx_w[:, e, k, m * P:(m + 1) * P],
                                           xm[:, e % 2, k, :], start=(e == 0 and k == 0),
                                           stop=(e == EX - 1 and k == KD - 1))
                    mm.then_inc(S["h_done"], 1)
                if hf == 0:
                    for b in (TB - 2, TB - 1):
                        turn(b, S["n0"], S["a_t0"], S["t0"], x1, 2 + b % 2)

            def router(b):
                pe.wait_ge(S["a_t1"], b + 1)
                for k in range(KD):
                    mm = pe.matmul(ps[:, 7, b * NE:(b + 1) * NE], x2T[:, k, b * P:(b + 1) * P], gate_w[:, k, :],
                                   start=(k == 0), stop=(k == KD - 1))
                mm.then_inc(S["lg_done"], 1)

            pe.wait_ge(S["ld_rt"], 32)
            for b in range(TB):
                pe.wait_ge(S["v_gm"], (b // 4) * EX + EX)
                if b >= 4:
                    pe.wait_ge(S["r1"], b - 3)
                else:
                    pe.wait_ge(S["v_g"], 1)
                for e in range(EX):
                    for k in range(KD):
                        mm = pe.matmul(ps[:, o1_bank(b), 0:D], gm[b // 4][:, e, k, (b % 4) * P:(b % 4) * P + P],
                                       ctx_w[:, e, k, :], start=(e == 0 and k == 0),
                                       stop=(e == EX - 1 and k == KD - 1))
                mm.then_inc(S["o1"], 1)
                if b >= 2:
                    turn(b - 2, S["n1"], S["a_t1"], S["t1"], x2, t1_bank(b - 2))
                if b == 3:
                    pe.wait_ge(S["v_g"], 2)
                if b >= 3:
                    router(b - 3)

            def hidden(n, par, hf, c):
                if isinstance(n, int) and n < 2:
                    j = 2 * n + hf
                    if 3 * j + c >= 4:
                        i, t = divmod(3 * j + c - 4, 3)
                        pe.wait_ge(*hidden_read(i, t))
                else:
                    i, t = divmod(3 * hf + c - 4 + 12, 3)
                    ge(pe, *hidden_read(n * 2 + (i - 4), t))
                bank = (3 * (2 * par + hf) + c) % 4
                lo, hi = GU[c]
                i = 0
                for k in range(KD):
                    w = slice(k * GW + lo, k * GW + hi)
                    for wp, xp in ((e_hi, x_hi), (e_hi, x_lo), (e_lo, x_hi)):
                        mm = pe.matmul(ps[0:hi - lo, bank, :], wp[:, par, w], xp[:, k, hf * 512:(hf + 1) * 512],
                                       start=(i == 0), stop=(i == 5))
                        i += 1
                mm.then_inc(S["gu_done"], 1)

            def down(n, par, first, hf):
                ge(pe, S["v_lo"], n * 4 + 2 * hf + 2)
                if first and hf == 1:
                    pe.wait_ge(S["v_ct"], 1)
                for b in range(4 * hf, 4 * hf + 4):
                    t = slice((b % 4) * P, (b % 4) * P + P)
                    main = slice(KD * GW, KD * GW + D)
                    tail = slice(KD * GW + D, KD * GW + 2 * D)
                    ops = [(a_hi[hf][:, t], e_hi[:, par, main]), (a_hi[hf][:, t], e_lo[:, par, main]),
                           (a_lo[hf][:, t], e_hi[:, par, main])]
                    ops += [(h_tail[:, hf, t], e[0:UP + FT, par, tail]) for e in (e_hi, e_lo)]
                    for i, (h, w) in enumerate(ops):
                        mm = pe.matmul(ps[:, 4 + b // 2, (b % 2) * D:(b % 2) * D + D], h, w,
                                       start=(first and b % 2 == 0 and i == 0), stop=False,
                                       skip_group_check=True)
                    mm.then_inc(S["dn_done"], 1)

            def expert(n, par, first):
                ge(pe, S["p_ex"], n * 2 + 2)
                for hf in range(2):
                    if first and hf:
                        pe.wait_ge(S["v_t1"], 4)
                    for c in range(3):
                        if not (first and hf == 0):
                            hidden(n, par, hf, c)
                        if first and hf and c == 0:
                            pe.wait_ge(S["v_comb"], 1)
                            pe.transpose(ps[:, 7, 0:NE * TB], comb.rearrange("p e b -> p (e b)"),
                                         ident[:, :]).then_inc(S["s_ct"], 1)
                    if hf == 1:
                        down(n, par, first, 0)
                    elif not first:
                        down(n - 1, 1 - par, isinstance(n, int) and n == 1, 1)

            pe.wait_ge(S["r1"], TB - 2)
            pe.wait_ge(S["v_t1"], 2)
            pe.wait_ge(S["p_ex"], 2)
            hidden(0, 0, 0, 0)
            turn(TB - 2, S["n1"], S["a_t1"], S["t1"], x2, t1_bank(TB - 2))
            turn(TB - 1, S["n1"], S["a_t1"], S["t1"], x2, t1_bank(TB - 1))
            router(TB - 3)
            hidden(0, 0, 0, 1)
            router(TB - 2)
            router(TB - 1)
            pe.wait_ge(S["a_t1"], TB - 3)
            hidden(0, 0, 0, 2)
            pe.wait_ge(S["r1"], TB)
            pe.wait_ge(S["p_tail"], 1)
            experts(pe, expert)
            down(ME - 1, 0, False, 1)

        @block.scalar
        def _(act):
            act.wait_ge(S["z_const"], 9)
            act.preload_act_table_set("natural_log_exp_and_others")
            act.wait_ge(S["ld_c"], 48)
            act.activation(head_c[:, 2:3], head_c[:, 1:2], ACT.Exp).then_inc(S["a_dt"], 1)
            act.wait_ge(S["a_dt"], 1)
            act.wait_ge(ld_w[0], 16)
            act.activation(w_hi[:, 0, :], w_raw[:, 0, 0:KD * PW], ACT.Copy).then_inc(S["w_split"], 1)
            def softplus(i):
                dt_ps = ps[0:H, 4:6, :].rearrange("p a t -> p (a t)")
                if i == 0:
                    act.wait_ge(S["s_dt"], 1)
                    act.activation(dt_e, dt_ps, ACT.Abs, bias=head_c[:, 0:1]).then_inc(S["a_dt"], 1)
                elif i == 1:
                    act.activation(dt_l, dt_ps, ACT.Relu, bias=head_c[:, 0:1]).then_inc(S["a_dt"], 1)
                elif i == 2:
                    act.wait_ge(S["a_dt"], 3)
                    act.activation(dt_e, dt_e, ACT.Exp, scale=-1.0).then_inc(S["a_dt"], 1)
                else:
                    act.wait_ge(S["a_dt"], 4)
                    act.activation(dt_ch, dt_e, ACT.Ln, bias=1.0).then_inc(S["a_dt"], 1)

            def step(n, par, front, mid, tail):
                q, qp, r = n - 1, 1 - par, n - 2

                def silu(p, pp, tile):
                    ge(act, S["v_tap"], p * TAP_N + TAP_AT[tile + 1])
                    act.activation(conv[:, pp, tile, :], conv[:, pp, tile, :], ACT.Silu).then_inc(S["a_silu"], 1)

                def z(hf):
                    ge(act, S["u_done"], q * 12 + 2 * NCONV + hf + 1)
                    if not (isinstance(q, int) and q < 2):
                        ge(act, S["p_y"], q * 2 - 2)
                    act.activation(z_gate[:, qp, hf * 512:(hf + 1) * 512], ps[:, (2 * NCONV + hf) % 4, :], ACT.Silu
                                   ).then_inc(S["a_z"], 1)

                def copy(j):
                    tile, hf = j // 2, j % 2
                    ge(act, S["u_done"], n * 12 + j + 1)
                    if j == 0 and not (isinstance(n, int) and n < 2):
                        ge(act, S["s_done"], n * UNITS - UNITS)
                    tap = KD * PW + tile * TAPS + TAPS - 1
                    act.activation(conv[:, par, tile, hf * 512:(hf + 1) * 512], ps[:, j % 4, :], ACT.Copy,
                                   scale=w_raw[:, par, tap:tap + 1]).then_inc(S["a_copy"], 1)

                def exp_decay(b):
                    ge(act, S["p_arg"], q * 3 * NB + 3 * b + 3)
                    d = decay[:, 2 * (b % 2):2 * (b % 2) + 2, :]
                    act.activation(d, d, ACT.Exp).then_inc(S["a_decay"], 1)

                def square(p, g):
                    ge(act, S["y_done"], p * UNITS + 4 * g + 4)
                    ge(act, S["ms_done"], p * 2 + g)
                    act.activation(y_sq[:, :], ps[:, 6 + g, :], ACT.Square).then_inc(S["a_sq"], 1)

                def rsqrt(p, g):
                    ge(act, S["ms_done"], p * 2 + g + 1)
                    ge(act, S["p_y"], p * 2)
                    act.activation(y_rs[:, g, :], ps[:, 6 + g, :], ACT.Ln, bias=eps_rms[:, 0:1]).then_inc(S["a_ln"], 1)
                    ge(act, S["a_ln"], p * 2 + g + 1)
                    act.activation(y_rs[:, g, :], y_rs[:, g, :], ACT.Exp, scale=-0.5).then_inc(S["a_rs"], 1)

                if mid:
                    z(0)
                    z(1)
                work = [[] for _ in range(2 * NTILE)]
                if isinstance(n, int) and n == 0:
                    work[0] += [lambda: softplus(0)]
                    work[1] += [lambda: softplus(1), lambda: softplus(2)]
                    work[2] += [lambda: softplus(3)]
                if mid:
                    work[0] += [lambda: silu(q, qp, 4)]
                if tail:
                    work[1] += [lambda: square(r, 1)]
                if mid or tail:
                    work[1] += [lambda: act.preload_act_table_set("natural_log_exp_and_others")]
                if mid:
                    for b, j in enumerate((2, 4, 6, 8)):
                        work[j] += [lambda b=b: exp_decay(b)]
                    work[8].insert(0, lambda: square(q, 0))
                if tail:
                    work[3] += [lambda: rsqrt(r, 0)]
                    work[5] += [lambda: rsqrt(r, 1)]
                for j in range(2 * NTILE):
                    if front and j < 2 * NCONV:
                        copy(j)
                    for f in work[j]:
                        f()
                if front:
                    act.preload_act_table_set("silu_and_others")
                    for tile in range(4):
                        silu(n, par, tile)

            steps(act, step)

            def layer_norm_scale(b, i):
                act.wait_ge(S[f"s{i}"], b + 1)
                act.activation(ln_v[:, b % 2, 0:1], ln_m[:, b % 2, 1:2], ACT.Ln, bias=eps_ln[:, 0:1]
                               ).then_inc(S[f"l{i}"], 1)
                act.wait_ge(S[f"l{i}"], b + 1)
                act.activation(ln_v[:, b % 2, 1:2], ln_v[:, b % 2, 0:1], ACT.Exp, scale=-0.5
                               ).then_inc(S[f"q{i}"], 1)

            def take_turned(b, t_sem, a_sem, dst, bank):
                act.wait_ge(t_sem, b + 1)
                act.activation(dst[:, :, b * P:(b + 1) * P],
                               ps[:, bank, 0:D].rearrange("p (k t) -> p k t", k=KD), ACT.Copy
                               ).then_inc(a_sem, 1)

            for b in range(TB):
                layer_norm_scale(b, 0)
                if b >= 2:
                    take_turned(b - 2, S["t0"], S["a_t0"], x1T, 2 + b % 2)
            take_turned(TB - 2, S["t0"], S["a_t0"], x1T, 2)
            take_turned(TB - 1, S["t0"], S["a_t0"], x1T, 3)

            act.preload_act_table_set("silu_and_others")
            for hf in range(2):
                act.wait_ge(S["h_done"], hf * EX + EX)
                if hf:
                    act.wait_ge(S["v_g"], hf)
                act.activation(sg_sb[:, :, :], ps[:, 4 + 2 * hf:6 + 2 * hf, :], ACT.Silu).then_inc(S["a_sg"], 1)
            act.preload_act_table_set("natural_log_exp_and_others")
            for b in range(TB):
                layer_norm_scale(b, 1)
                if b >= 2:
                    take_turned(b - 2, S["t1"], S["a_t1"], x2T, t1_bank(b - 2))
            take_turned(TB - 2, S["t1"], S["a_t1"], x2T, t1_bank(TB - 2))
            take_turned(TB - 1, S["t1"], S["a_t1"], x2T, t1_bank(TB - 1))

            act.wait_ge(S["v_rt"], 4)
            act.activation(ew, ew, ACT.Exp).then_inc(S["a_el"], 1)

            act.preload_act_table_set("silu_and_others")

            def expert(n, par, first):
                def silu_gate(hf, tail):
                    ge(act, S["gu_done"], n * 6 + 3 * hf + (3 if tail else 1))
                    if not first:
                        ge(act, S["v_lo"], n * 4 + 2 * hf - 3 + tail)
                    bank = (3 * (2 * par + hf) + 2 * tail) % 4
                    dst = h_b[UP:UP + FT, hf, :] if tail else h_a[:, hf, :]
                    act.activation(dst, ps[0:FT, bank, :] if tail else ps[:, bank, :], ACT.Silu
                                   ).then_inc(S["a_s"], 1)

                def high(hf, tail):
                    if first:
                        act.wait_ge(S["v_t"], 2 * hf + 1 + tail)
                    else:
                        ge(act, S["v_w"], n * 4 - 4 + 2 * hf + 1 + tail)
                        ge(act, S["dn_done"], n * TB + 4 * hf - 4)
                    src, dst = ((h_b[UP:UP + FT, hf, :], h_tail[UP:UP + FT, hf, :]) if tail else
                                (h_a[:, hf, :], a_hi[hf]))
                    act.activation(dst, src, ACT.Copy).then_inc(S["a_hi"], 1)
                for hf in range(2):
                    for tail in (0, 1):
                        silu_gate(hf, tail)
                        high(hf, tail)
            act.wait_ge(S["o1"], TB)
            experts(act, expert)

            act.preload_act_table_set("natural_log_exp_and_others")
            for b in range(TB):
                layer_norm_scale(b, 2)

        @block.vector
        def _(dve):
            dve.wait_ge(S["ld_x"], 16)
            dve.tensor_copy(x_hi[:, :, :], xT_raw).then_inc(S["d_x"], 1)
            dve.wait_ge(S["d_x"], 1)
            dve.tensor_tensor(x_lo[:, :, :], xT_raw, x_hi[:, :, :].bitcast(F32), ALU.subtract).then_inc(S["d_x"], 1)
            dve.wait_ge(S["w_split"], 1)
            dve.tensor_tensor(w_lo[:, 0, :], w_raw[:, 0, 0:KD * PW], w_hi[:, 0, :].bitcast(F32), ALU.subtract
                              ).then_inc(S["w_split"], 1)
            def sum_dt():
                made = [0]

                def link(ins):
                    made[0] += 1
                    ins.then_inc(S["d_dt"], 1)
                    dve.wait_ge(S["d_dt"], made[0])
                dve.wait_ge(S["a_dt"], 5)
                link(dve.tensor_tensor(dt_l, dt_l, dt_ch, ALU.add))
                link(dve.tensor_scalar(dt_da, dt_l, head_c[:, 2:3], -1.0, ALU.mult, ALU.mult))
                for b in range(NB):
                    t = slice(b * T, (b + 1) * T)
                    ins = dve.tensor_tensor_scan(dt_cum[:, t], one[:, :].broadcast_to([H, T]), dt_da[:, t], 0.0, ALU.mult, ALU.add)
                link(ins)

            def take_dt():
                dve.wait_ge(S["s_dtT"], 1)
                dve.tensor_copy(dt_tok[:, :, :], ps[:, 4, 0:TB * H].rearrange("p (b h) -> p b h", b=TB))
                dve.tensor_copy(cum_tok[:, :, :], ps[:, 5, 0:TB * H].rearrange("p (b h) -> p b h", b=TB)
                                ).then_inc(S["d_dtT"], 1)
                dve.wait_ge(S["d_dtT"], 1)

            def step(n, par, front, mid, tail):
                q, qp, r, rp = n - 1, 1 - par, n - 2, par

                def x_scaled(c):
                    ge(dve, S["xt_done"], q * 2 + c + 1)
                    ge(dve, S["y_done"], q * UNITS)
                    dve.tensor_tensor(xs[:, 4 * c:4 * c + 4, :].rearrange("p b (h c) -> p b h c", h=2),
                                      ps[:, 4 + c, :].rearrange("p (b h c) -> p b h c", b=4, h=2),
                                      dt_tok[:, 4 * c:4 * c + 4, bass.ds(q * 2, 2)].unsqueeze(3)
                                      .broadcast_to([P, 4, 2, HP]), ALU.mult).then_inc(S["v_xs"], 1)

                def weigh(k):
                    ge(dve, S["a_decay"], q * NB + k // 2 + 1)
                    ge(dve, S["s_done"], q * UNITS + k + 1)
                    ge(dve, S["y_done"], q * UNITS + max(k - 1, 0))
                    dve.tensor_tensor(scores[:, k % 2, :], ps[:, 4 + k % 2, 0:SC], decay[:, k % 4, :], ALU.mult
                                      ).then_inc(S["v_m"], 1)

                def tap(m, i):
                    halves, s = TAPS_OF[m][i]
                    if s == 1:
                        ge(dve, S["a_copy"], n * (2 * NCONV) + 2 * m + halves.stop)
                    else:
                        before = max(k for k in range(i) if TAPS_OF[m][k][1] == s - 1 and
                                     TAPS_OF[m][k][0].stop >= halves.stop)
                        ge(dve, S["v_tap"], n * TAP_N + TAP_AT[m] + before + 1)
                    o = conv[:, par, m, :].rearrange("p (b t) -> p b t", b=NB)[:, 2 * halves.start:2 * halves.stop, :]
                    u = ps[:, (2 * m) % 4:(2 * m) % 4 + 2, :].rearrange("p a (b t) -> p (a b) t", b=2)
                    u = u[:, 2 * halves.start:2 * halves.stop, :]
                    c = KD * PW + m * TAPS + TAPS - 1 - s
                    dve.scalar_tensor_tensor(out=o[:, :, s:], in0=u[:, :, 0:T - s],
                                             scalar=w_raw[:, par, c:c + 1], in1=o[:, :, s:],
                                             op0=ALU.mult, op1=ALU.add).then_inc(S["v_tap"], 1)

                def gate(p, pp, g):
                    ge(dve, S["a_z"], p * 2 + g + 1)
                    ge(dve, S["a_sq"], p * 2 + g + 1)
                    dve.tensor_tensor(z_gate[:, pp, g * 512:(g + 1) * 512], ps[:, 6 + g, :], z_gate[:, pp, g * 512:(g + 1) * 512],
                                      ALU.mult).then_inc(S["v_yz"], 1)

                between = {}
                if mid:
                    between[0, 3] = [lambda: x_scaled(0)]
                    between[0, 5] = [lambda: x_scaled(1)]
                    for k, at_ in enumerate(((1, 0), (2, 0), (2, 1), (3, 0), (3, 1), (4, 0), (4, 1), (4, 3))):
                        between[at_] = [lambda k=k: weigh(k)]
                    between[4, 2] = [lambda: gate(q, qp, 0)]
                if tail:
                    between[0, 4] = [lambda: gate(r, rp, 1)]
                if isinstance(n, int) and n == 0:
                    between[1, 0] = [sum_dt]
                for m in range(NCONV):
                    for i in range(len(TAPS_OF[m])):
                        for f in between.get((m, i), []):
                            f()
                        if front:
                            tap(m, i)
            steps(dve, step, take_dt)

            def ln_front(b, i, src, res):
                r = ln_r[:, b % 2, :]
                if i < 2:
                    dve.wait_ge(S[f"o{i}"], b + 1)
                else:
                    dve.wait_ge(S["dn_done"], (ME - 1) * TB + (b // 2) * 2 + 2)
                if b >= 2:
                    dve.wait_ge(S[f"n{i}"], b - 1)
                dve.tensor_tensor(r, src, res, ALU.add).then_inc(S[f"r{i}"], 1)
                dve.wait_ge(S[f"r{i}"], b + 1)
                stat(dve.bn_stats(ln_s[:, b % 2, :], r))
                dve.bn_aggr(ln_m[:, b % 2, :], ln_s[:, b % 2, :]).then_inc(S[f"s{i}"], 1)

            def ln_back(b, i, dst):
                dve.wait_ge(S[f"q{i}"], b + 1)
                dve.wait_ge(S[f"s{i}"], b + 1)
                dve.tensor_scalar(dst, ln_r[:, b % 2, :], ln_m[:, b % 2, 0:1], ln_v[:, b % 2, 1:2],
                                  ALU.subtract, ALU.mult).then_inc(S[f"n{i}"], 1)
            stats = [0]

            def stat(ins):
                stats[0] += 1
                ins.then_inc(S["ln_st"], 1)
                dve.wait_ge(S["ln_st"], stats[0])

            def mask_x(i):
                hf, e = i // EX, i % EX
                if i == 0:
                    dve.wait_ge(S["p_mask"], 6)
                dve.wait_ge(S["a_t0"], 4 * hf + 4)
                if i >= 2:
                    dve.wait_ge(S["h_done"], i - 1)
                t = slice(hf * 512, (hf + 1) * 512)
                dve.tensor_tensor(xm[:, e % 2, :, :], x1T[:, :, t],
                                  emask[:, e, t].unsqueeze(1).broadcast_to([P, KD, 512]), ALU.mult
                                  ).then_inc(S["v_xm"], 1)

            def gate_g(hf):
                dve.wait_ge(S["a_sg"], hf + 1)
                if hf:
                    dve.wait_ge(S["v_gm"], EX)
                dve.tensor_tensor(g_sb, sg_sb, ps[:, 4 + 2 * hf:6 + 2 * hf, :], ALU.mult).then_inc(S["v_g"], 1)
                dve.wait_ge(S["v_g"], hf + 1)

            def mask_g(hf, e):
                t = slice(hf * 512, (hf + 1) * 512)
                dve.tensor_tensor(gm[hf][:, e, :, :], g_sb,
                                  emask[:, e, t].unsqueeze(1).broadcast_to([P, KD, 512]), ALU.mult
                                  ).then_inc(S["v_gm"], 1)

            dve.wait_ge(S["ld_xt"], 16)
            for b in range(TB):
                if b == TB - 1:
                    mask_x(0)
                    mask_x(1)
                ln_front(b, 0, ps[:, b % 2, 0:D], x_tok[:, b, :])
                if b >= 1:
                    ln_back(b - 1, 0, x1[:, b - 1, :])
            ln_back(TB - 1, 0, x1[:, TB - 1, :])
            for i in range(2, 6):
                mask_x(i)
            gate_g(0)
            mask_x(6)
            mask_g(0, 0)
            mask_x(7)
            for e in range(1, EX):
                mask_g(0, e)
            gate_g(1)
            for e in range(EX):
                mask_g(1, e)

            def split_x2(hf):
                t = slice(hf * 512, (hf + 1) * 512)
                dve.wait_ge(S["a_t1"], 4 * hf + 4)
                dve.tensor_copy(x_hi[:, :, t], x2T[:, :, t]).then_inc(S["v_t1"], 1)
                dve.wait_ge(S["v_t1"], 2 * hf + 1)
                dve.tensor_tensor(x_lo[:, :, t], x2T[:, :, t], x_hi[:, :, t].bitcast(F32), ALU.subtract
                                  ).then_inc(S["v_t1"], 1)

            for b in range(TB):
                ln_front(b, 1, ps[:, o1_bank(b), 0:D], x1[:, b, :])
                if b >= 1:
                    ln_back(b - 1, 1, x2[:, b - 1, :])
                if b == TB - 2:
                    split_x2(0)
            ln_back(TB - 1, 1, x2[:, TB - 1, :])
            split_x2(1)

            made = [0]

            def rlink(ins):
                made[0] += 1
                ins.then_inc(S["v_rt"], 1)
                dve.wait_ge(S["v_rt"], made[0])
            dve.wait_ge(S["lg_done"], TB)
            dve.wait_ge(S["ld_rt"], 32)
            lg = ps[:, 7, 0:TB * NE].rearrange("p (b e) -> p b e", b=TB)
            dve.tensor_copy(logit, lg).then_inc(S["v_rt"], 1)
            dve.tensor_tensor(biased[:, :, 0:NE], lg, eb_sb.unsqueeze(1).broadcast_to([P, TB, NE]), ALU.add
                              ).then_inc(S["v_rt"], 1)
            made[0] = 2
            dve.wait_ge(S["v_rt"], 2)
            rlink(dve.tensor_reduce(lmax, logit, AX.X, ALU.max))
            rlink(dve.tensor_tensor(ew, logit, lmax.unsqueeze(2).broadcast_to([P, TB, NE]), ALU.subtract))
            rlink(dve.memset(biased[:, :, NE:NBI], PAD))
            for b in range(TB):
                ins = dve.max(top8[:, b, :], biased[:, b, 0:NE])
            rlink(ins)
            rlink(dve.memset(top8[:, :, 2:8], PAD))
            for b in range(TB):
                ins = dve.match_replace(out=taken[:, b, :], in_to_replace=top8[:, b, :],
                                        in_values=biased[:, b, :], imm_value=HIT)
            rlink(ins)
            rlink(dve.tensor_tensor(taken[:, :, 0:NE], taken[:, :, 0:NE], biased[:, :, 0:NE], ALU.not_equal))
            dve.wait_ge(S["a_el"], 1)
            rlink(dve.tensor_tensor(ew, ew, taken[:, :, 0:NE], ALU.mult))
            rlink(dve.tensor_reduce(lsum, ew, AX.X, ALU.add))
            rlink(dve.reciprocal(lrec, lsum))
            dve.tensor_tensor(comb.rearrange("p e b -> p b e"), ew,
                              lrec.unsqueeze(2).broadcast_to([P, TB, NE]), ALU.mult).then_inc(S["v_comb"], 1)

            def expert(n, par, first):
                for hf in range(2):
                    for tail in (0, 1):
                        bank = (3 * (2 * par + hf) + 1 + tail) % 4
                        h = h_b[UP:UP + FT, hf, :] if tail else h_a[:, hf, :]
                        up = ps[UP:UP + FT, bank, :] if tail else ps[:, bank, :]
                        ge(dve, S["gu_done"], n * 6 + 3 * hf + 2 + tail)
                        ge(dve, S["a_s"], n * 4 + 2 * hf + 1 + tail)
                        dve.tensor_tensor(h, h, up, ALU.mult).then_inc(S["v_t"], 1)
                        if not first:
                            ge(dve, S["v_t"], n * 4 + 2 * hf + 1 + tail)
                            if hf == 0 and tail == 0:
                                ge(dve, ld_cb[par], n * 8 + (8 if par else 0))
                            w = comb_b[UP:UP + FT, par, :] if tail else comb_b[:, par, :]
                            dve.tensor_tensor(h, h, w[:, hf * 512:(hf + 1) * 512], ALU.mult
                                              ).then_inc(S["v_w"], 1)
                        ge(dve, S["a_hi"], n * 4 + 2 * hf + 1 + tail)
                        if tail and first and hf == 0:
                            dve.wait_ge(S["p_tail"], 1)
                        hi, lo = ((h_tail[UP:UP + FT, hf, :], h_tail[0:FT, hf, :]) if tail else
                                  (a_hi[hf], a_lo[hf]))
                        dve.tensor_tensor(lo, h, hi.bitcast(F32), ALU.subtract).then_inc(S["v_lo"], 1)
                        if first and hf == 0 and not tail:
                            dve.wait_ge(S["s_ct"], 1)
                            dve.tensor_copy(comb_t, ps[:, 7, 0:NE * TB]).then_inc(S["v_ct"], 1)
            experts(dve, expert)
            for b in range(TB):
                ln_front(b, 2, ps[:, 4 + b // 2, (b % 2) * D:(b % 2) * D + D], x2[:, b, :])
                if b >= 1:
                    ln_back(b - 1, 2, x1[:, b - 1, :])
            ln_back(TB - 1, 2, x1[:, TB - 1, :])



_OUT = (NB, T, D)


def kernel(**inputs):
    import numpy as np
    import concourse.bacc as bacc
    from concourse.bass_utils import run_bass_kernel_spmd

    g = {k: np.asarray(v) for k, v in inputs.items()}
    x = g["x"].reshape(NT, D)
    win = g["L0_attn_Win"]
    o_z, o_b, o_c, o_dt = H * HP, 2 * H * HP, 2 * H * HP + H * N, 2 * H * HP + 2 * H * N

    def rows(i):
        t = [win[P * i:][:P]]
        for h in (2 * i, 2 * i + 1):
            t += [win[o_b + N * h:][:N], win[o_c + N * h:][:N]]
        t += [win[o_z + P * i:][:P]]
        return np.concatenate(t, 0)
    cx = g["L0_attn_conv_w_x"].reshape(NPAIR, P, TAPS)
    cb, cc = g["L0_attn_conv_w_b"], g["L0_attn_conv_w_c"]
    pairs = []
    for i in range(NPAIR):
        w = rows(i).T.reshape(KD, P, PW).transpose(1, 0, 2).reshape(P, KD * PW)
        taps = [cx[i], cb[2 * i], cc[2 * i], cb[2 * i + 1], cc[2 * i + 1]]
        pairs.append(np.concatenate([w] + taps, 1))
    wg = np.concatenate([g["L0_ffn_sw_gate"][None], g["L0_ffn_w_gate"]], 0)
    wu = np.concatenate([g["L0_ffn_sw_up"][None], g["L0_ffn_w_up"]], 0)
    wd = np.concatenate([g["L0_ffn_sw_down"][None], g["L0_ffn_w_down"]], 0)
    gu = np.zeros((ME, GW, D), wg.dtype)
    gu[:, 0:P], gu[:, P:2 * P] = wg[:, :P], wu[:, :P]
    gu[:, 2 * P:2 * P + FT], gu[:, 2 * P + UP:GW] = wg[:, P:], wu[:, P:]
    gu = gu.transpose(0, 2, 1).reshape(ME, KD, P, GW).transpose(0, 2, 1, 3).reshape(ME, P, KD * GW)
    wd = wd.transpose(0, 2, 1)
    dn = np.zeros((ME, P, 2 * D), wd.dtype)
    dn[:, :, :D] = wd[:, :P]
    dn[:, :FT, D:] = dn[:, UP:UP + FT, D:] = wd[:, P:]
    arrays = {
        "xT": x.T, "x": x, "winT": np.stack(pairs), "wdtT": win[o_dt:].T,
        "a_log": g["L0_attn_A_log"], "dt_bias": g["L0_attn_dt_bias"], "woutT": g["L0_attn_Wout"].T,
        "ids": g["itok_BxS_13_99985"].reshape(NT), "ctxT": g["ctx_2048"].transpose(0, 2, 1),
        "gateT": g["L0_ffn_gate_w"].T, "ebias": g["L0_ffn_expert_bias"],
        "wexp": np.concatenate([gu, dn], 2),
    }
    arrays = {f"in_{k}": np.ascontiguousarray(v) for k, v in arrays.items()}
    nc = bacc.Bacc("TRN2", target_bir_lowering=False, num_devices=1)
    args = [nc.dram_tensor(n, a.shape, mybir.dt.from_np(a.dtype), kind="ExternalInput").ap()
            for n, a in arrays.items()]
    out = nc.dram_tensor("out", (NT, D), F32, kind="ExternalOutput").ap()
    build_layer(nc, *args, out)
    r = run_bass_kernel_spmd(nc, [arrays], core_ids=[0])
    return r.results[0]["out"].reshape(_OUT)
```
